# Optimizing a Trainium2 kernel written in Bass

```python
import numpy as np
import jax
import jax.numpy as jnp

def _softmax(x, axis=-1):
    return jax.nn.softmax(x, axis=axis)
def _gelu(x):
    return jax.nn.gelu(x, approximate=True)
def _silu(x):
    return jax.nn.silu(x)
def _sigmoid(x):
    return jax.nn.sigmoid(x)
def _layernorm(x, axis=-1, eps=1e-5):
    m = jnp.mean(x, axis=axis, keepdims=True)
    v = jnp.var(x, axis=axis, keepdims=True)
    return (x - m) / jnp.sqrt(v + eps)
def _scatter_add(tgt, idx, src, axis=0):
    return tgt.at[idx].add(src)
def _segment_sum(src, seg, n):
    return jax.ops.segment_sum(src, seg, n)

kernel_name = 'mk_conv_attn_hybrid_d2_conv_nchw128_cc7736'

def setup_inputs(seed: int = 0):
    np.random.seed(seed)
    _w = jnp.asarray
    def _rec_inputs():
        import jax
        import jax.numpy as jnp
        _gk = jax.random.key(seed)
        x = -0.0002928 + 1 * jax.random.normal(jax.random.fold_in(_gk, 1), (32, 128, 32, 32), jnp.float32)
        return x
    x = _rec_inputs()
    def _L0_conv_setup():
        import jax, jax.numpy as jnp
        import numpy as np
        PAD = 1
        key = jax.random.key(seed)
        k1, k2, k3 = jax.random.split(key, 3)
        N, C, F, H, W, HH, WW = (32, 128, 128, 32, 32, 3, 3)
        x = jax.random.normal(k1, (N, C, H, W), dtype=jnp.float32)
        weight = jax.random.normal(k2, (F, C, HH, WW), dtype=jnp.float32) * 0.05
        bias = jax.random.normal(k3, (F,), dtype=jnp.float32) * 0.05
        return {'x': x, 'weight': weight, 'bias': bias}
    _L0_conv_all = _L0_conv_setup()
    _L0_conv_in = {k: v for k, v in _L0_conv_all.items() if k in ('weight', 'bias', )}
    del _L0_conv_all

    def _L1_attn_setup():
        import jax, jax.numpy as jnp
        import numpy as np
        SCALE = 0.1
        TEMP = 0.5
        EPS = 1e-06
        key = jax.random.key(seed)
        k1, = jax.random.split(key, 1)
        x = jax.random.normal(k1, (4, 4096, 128), dtype=jnp.float32)
        ln_weight = jnp.ones((128,), dtype=jnp.float32)
        ln_bias = jnp.zeros((128,), dtype=jnp.float32)
        return {'x': x, 'ln_weight': ln_weight, 'ln_bias': ln_bias}
    _L1_attn_all = _L1_attn_setup()
    _L1_attn_in = {k: v for k, v in _L1_attn_all.items() if k in ('ln_weight', 'ln_bias', )}
    del _L1_attn_all

    def _L1_ffn_setup():
        import jax, jax.numpy as jnp
        import numpy as np
        B, N, D, C, E, K = (8, 8192, 128, 128, 8, 2)
        key = jax.random.key(seed)
        k0, k1, k2 = jax.random.split(key, 3)
        x = jax.random.normal(k0, (B, N, D), dtype=jnp.float32)
        router_w = jax.random.normal(k1, (D, E), dtype=jnp.float32) * 0.05
        router_b = jnp.zeros((E,), dtype=jnp.float32)
        expert_w = jax.random.normal(k2, (E, D, C), dtype=jnp.float32) * (1.0 / np.sqrt(D))
        expert_b = jnp.zeros((E, C), dtype=jnp.float32)
        return {'x': x, 'router_w': router_w, 'router_b': router_b, 'expert_w': expert_w, 'expert_b': expert_b}
    _L1_ffn_all = _L1_ffn_setup()
    _L1_ffn_in = {k: v for k, v in _L1_ffn_all.items() if k in ('router_w', 'router_b', 'expert_w', 'expert_b', )}
    del _L1_ffn_all

    return {
        "x": x,
        "L0_conv_weight": _L0_conv_in["weight"],
        "L0_conv_bias": _L0_conv_in["bias"],
        "L1_attn_ln_weight": _L1_attn_in["ln_weight"],
        "L1_attn_ln_bias": _L1_attn_in["ln_bias"],
        "L1_ffn_router_w": _L1_ffn_in["router_w"],
        "L1_ffn_router_b": _L1_ffn_in["router_b"],
        "L1_ffn_expert_w": _L1_ffn_in["expert_w"],
        "L1_ffn_expert_b": _L1_ffn_in["expert_b"],
    }

def reference(x, L0_conv_weight, L0_conv_bias, L1_attn_ln_weight, L1_attn_ln_bias, L1_ffn_router_w, L1_ffn_router_b, L1_ffn_expert_w, L1_ffn_expert_b):
    import jax
    import jax.numpy as jnp
    def _L0_conv_ref(x, weight, bias):
        import jax, jax.numpy as jnp
        import numpy as np
        PAD = 1
        N, C, H, W = x.shape
        F, _, HH, WW = weight.shape
        pad = PAD
        out_H = H - HH + 1 + 2 * pad
        out_W = W - WW + 1 + 2 * pad
        HHH = max(out_H, HH)
        WWW = max(out_W, WW)
        init_H = H + 2 * pad + HHH - 1
        init_W = W + 2 * pad + WWW - 1
        xp = jnp.pad(x, ((0, 0), (0, 0), (pad, init_H - pad - H), (pad, init_W - pad - W)))
        wp = jnp.pad(weight, ((0, 0), (0, 0), (0, init_H - HH), (0, init_W - WW)))
        xf = jnp.fft.rfft2(xp)
        wf = jnp.fft.rfft2(wp)
        of = jnp.einsum('nchw,fchw->nfhw', xf, jnp.conj(wf))
        out = jnp.fft.irfft2(of, s=(init_H, init_W))[..., :out_H, :out_W]
        return out + bias[None, :, None, None]

    def _L1_attn_ref(x, ln_weight, ln_bias):
        import jax, jax.numpy as jnp
        import numpy as np
        SCALE = 0.1
        TEMP = 0.5
        EPS = 1e-06
        xn = x / jnp.maximum(jnp.linalg.norm(x, axis=-1, keepdims=True), 1e-12)
        sim = jnp.einsum('bnd,bmd->bnm', xn, xn) / TEMP
        sim = jax.nn.softmax(sim, axis=-1)
        sim = sim + jax.nn.softmax(sim, axis=-2)
        x_neg = jnp.einsum('bnm,bmd->bnd', sim, x)
        y = x - SCALE * x_neg
        mu = jnp.mean(y, axis=-1, keepdims=True)
        var = jnp.mean((y - mu) ** 2, axis=-1, keepdims=True)
        out = (y - mu) / jnp.sqrt(var + EPS) * ln_weight + ln_bias
        return out

    def _L1_ffn_ref(x, router_w, router_b, expert_w, expert_b):
        import jax, jax.numpy as jnp
        import numpy as np
        B, N, D, C, E, K = (8, 8192, 128, 128, 8, 2)
        router_probs = jax.nn.softmax(x @ router_w + router_b, axis=-1)
        top_p, top_i = jax.lax.top_k(router_probs, K)
        top_p = top_p / jnp.sum(top_p, axis=-1, keepdims=True)
        expert_out = jnp.einsum('bnd,edc->bnec', x, expert_w) + expert_b
        gathered = jnp.take_along_axis(expert_out, top_i[..., None], axis=2)
        return jnp.einsum('bnk,bnkc->bnc', top_p, gathered)

    def _gn(v, G=32, eps=1e-5):
        B_, C_, H_, W_ = v.shape
        g = v.reshape(B_, G, C_ // G, H_, W_)
        m = jnp.mean(g, axis=(2, 3, 4), keepdims=True)
        s = jnp.var(g, axis=(2, 3, 4), keepdims=True)
        return ((g - m) / jnp.sqrt(s + eps)).reshape(v.shape)

    def _ln_c(v, eps=1e-6):
        m = jnp.mean(v, axis=1, keepdims=True)
        s = jnp.var(v, axis=1, keepdims=True)
        return (v - m) / jnp.sqrt(s + eps)

    def _ln_t(v, eps=1e-5):
        m = jnp.mean(v, axis=-1, keepdims=True)
        s = jnp.var(v, axis=-1, keepdims=True)
        return (v - m) / jnp.sqrt(s + eps)

    def _to_tokens(v):
        B_, C_, H_, W_ = v.shape
        return v.reshape(B_, C_, H_ * W_).transpose(0, 2, 1)
    def _from_tokens(t, like):
        B_, C_, H_, W_ = like.shape
        return t.transpose(0, 2, 1).reshape(B_, C_, H_, W_)

    x = x + _L0_conv_ref(_gn(x), L0_conv_weight, L0_conv_bias)
    t = _to_tokens(x)
    t = t + _L1_attn_ref(_ln_t(t), L1_attn_ln_weight, L1_attn_ln_bias)
    t = t + _L1_ffn_ref(_ln_t(t), L1_ffn_router_w, L1_ffn_router_b, L1_ffn_expert_w, L1_ffn_expert_b)
    x = _from_tokens(t, x)
    return x


_drawn_inputs = setup_inputs


def setup_inputs(seed=0):
    import zlib

    import numpy as np

    out = dict(_drawn_inputs(seed))
    spreads = {'L1_attn_ln_weight': (1.0, 0.2),
     'L1_attn_ln_bias': (0.0, 0.1),
     'L1_ffn_router_b': (0.0, 0.1),
     'L1_ffn_expert_b': (0.0, 0.342)}
    factors = {}
    for name, (base, spread) in spreads.items():
        noise = np.random.default_rng([zlib.crc32(name.encode()), seed]).standard_normal(out[name].shape)
        drawn = base * np.exp(spread * noise) if base else spread * noise
        out[name] = jnp.asarray(drawn.astype(out[name].dtype))
    for name, factor in factors.items():
        out[name] = (out[name] * factor).astype(out[name].dtype)
    return out
```

```python
from contextlib import ExitStack

import concourse.bass as bass
from concourse import mybir

F32 = mybir.dt.float32
F32R = mybir.dt.float32r
U32 = mybir.dt.uint32
ALU = mybir.AluOpType
ACT = mybir.ActivationFunctionType

P = 128
KS = 3
HALF = 512
GN_EPS, LNT_EPS, ATTN_EPS = 1e-5, 1e-5, 1e-6
SCALE, INV_TEMP = 0.1, 2.0
CONV_MM = ((7, 7), (7, 6), (7, 6), (7, 7))
FIRST, STAGES_AHEAD, STAGES_BEHIND = -2, 2, 3


class Image:

    def __init__(self, pair, c):
        self.n = 2 * pair + c
        self.nth = pair + c // 2
        self.par = c % 2


class Iteration:

    def __init__(self, pair, c, images):
        self.pair, self.c, self.images = pair, c, images
        self.static = isinstance(pair, int)

    def image(self, d):
        if self.static and not 0 <= 2 * self.pair + self.c + d < self.images:
            return None
        return Image(self.pair, self.c + d)


def iterations(eng, images, run):
    last = images + STAGES_BEHIND
    begin = STAGES_BEHIND + 1
    pairs = (images - STAGES_AHEAD - begin) // 2
    for i in range(FIRST, begin):
        run(Iteration(0, i, images))
    with eng.Fori(0, pairs) as pair:
        run(Iteration(pair, begin, images))
        run(Iteration(pair, begin + 1, images))
    for i in range(begin + 2 * pairs, last):
        run(Iteration(0, i, images))


def build(nc, x, conv_w, conv_b, ln_w, ln_b, router_w, router_b, expert_w, expert_b,
          identity, group_mean, expert_ids, bias_rows, out):
    NB, C, HW = x.shape
    W = 32
    H = HW // W
    PW = W + 2
    T = HW // P
    NH = HW // HALF
    TPH = T // NH
    RPH = H // NH
    E = router_w.shape[1]
    TAPS = KS * KS
    STEPS = T

    with ExitStack() as ctx:
        def sb(name, shape, dt=F32):
            return ctx.enter_context(nc.sbuf_tensor(name, shape, dt))

        def psum(name, n=HALF):
            return ctx.enter_context(nc.psum_tensor(name, [P, n], F32))

        def sem(name):
            return ctx.enter_context(nc.semaphore(name))

        ident = sb("ident", [P, P])
        gmat = sb("gmat", [P, P])
        ids = sb("ids", [P, T, E])
        rows24 = sb("rows24", [3 * E, 2])
        cb = sb("cb", [P, 1])
        lnw = sb("lnw", [P, C])
        lnb = sb("lnb", [P, C])
        rb = sb("rb", [P, T, E])
        eb = sb("eb", [3 * E, C])
        ebt = sb("ebt", [3 * E, C])
        eblo = sb("eblo", [3 * E, C])
        ebhi = sb("ebhi", [3 * E, C], F32R)
        ebs = sb("ebs", [3 * E, C], F32R)
        rw = sb("rw", [P, E])
        rwhi = sb("rwhi", [P, E], F32R)
        rwlo = sb("rwlo", [P, E], F32R)
        cwhi = sb("cwhi", [P, TAPS, C], F32R)
        cwlo = sb("cwlo", [P, TAPS, C], F32R)
        ewhi = sb("ewhi", [P, E * C], F32R)
        ewlo = sb("ewlo", [P, E * C], F32R)
        nhalf = sb("nhalf", [P, 1])
        xc = [sb(f"xc_{p}", [P, HW]) for p in range(2)]
        gst = sb("gst", [P, NH, 6])
        gmv = sb("gmv", [P, 2])
        gmean = sb("gmean", [P, 1])
        gdev = sb("gdev", [P, 1])
        gv = sb("gv", [P, 1])
        gve = sb("gve", [P, 1])
        grs = sb("grs", [P, 1])
        gnhi = sb("gnhi", [P, H + 2, PW], F32R)
        gnlo = sb("gnlo", [P, H + 2, PW], F32R)
        x1c = sb("x1c", [P, HW])
        x1t = [sb(f"x1t_{p}", [P, T, C]) for p in range(2)]
        l1st = sb("l1st", [P, T, 6])
        l1mv = [sb(f"l1mv_{p}", [P, T, 2]) for p in range(2)]
        l1ve = sb("l1ve", [P, T])
        l1rs = [sb(f"l1rs_{p}", [P, T]) for p in range(2)]
        l1rec = sb("l1rec", [P, T])
        l1q = sb("l1q", [P, T])
        l1n = sb("l1n", [P, T])
        l1in = sb("l1in", [P, T])
        l1a = sb("l1a", [P, T])
        xnt = sb("xnt", [P, T, C])
        xnhi = [sb(f"xnhi_{p}", [P, HW], F32R) for p in range(2)]
        xnlo = [sb(f"xnlo_{p}", [P, HW], F32R) for p in range(2)]
        es = sb("es", [P, T, HW])
        rsum = [sb(f"rsum_{p}", [P, T]) for p in range(2)]
        rinv = sb("rinv", [P, T])
        rbc = sb("rbc", [P, HW])
        s1 = [sb(f"s1_{p}", [P, HW]) for p in range(2)]
        s1hi = [sb(f"s1hi_{p}", [P, HW], F32R) for p in range(2)]
        s1lo = [sb(f"s1lo_{p}", [P, HW], F32R) for p in range(2)]
        fx = [sb(f"fx_{p}", [P, HW]) for p in range(2)]
        hx = [sb(f"hx_{p}", [P, HW], F32R) for p in range(2)]
        csum = [sb(f"csum_{p}", [P, T]) for p in range(2)]
        ci = [sb(f"ci_{p}", [P, T]) for p in range(2)]
        ci1 = sb("ci1", [P, T])
        u = [sb(f"u_{p}", [P, T, C]) for p in range(2)]
        wf = sb("wf", [P, C])
        whi = [sb(f"whi_{p}", [P, C], F32R) for p in range(2)]
        wlo = [sb(f"wlo_{p}", [P, C], F32R) for p in range(2)]
        yhi = [sb(f"yhi_{p}", [P, C], F32R) for p in range(2)]
        x1b = [sb(f"x1b_{p}", [P, T, C]) for p in range(2)]
        ysum = sb("ysum", [P, 1])
        xneg = sb("xneg", [P, HW])
        yv = sb("yv", [P, T, C])
        gnf = yv[:].rearrange("p t c -> p (t c)")
        l2st = sb("l2st", [P, T, 6])
        l2mv = sb("l2mv", [P, T, 2])
        l2ve = sb("l2ve", [P, T])
        l2rs = sb("l2rs", [P, T])
        t1 = sb("t1", [P, T, C])
        l3st = sb("l3st", [P, T, 6])
        l3mv = sb("l3mv", [P, T, 2])
        l3ve = sb("l3ve", [P, T])
        l3rs = sb("l3rs", [P, T])
        zt = xnt
        zhi = sb("zhi", [P, HW], F32R)
        zlo = sb("zlo", [P, HW], F32R)
        lg = sb("lg", [P, T, E])
        mx = sb("mx", [P, T, 8])
        mi = sb("mi", [P, T, 8], U32)
        mf = sb("mf", [P, 2, T])
        gd = sb("gd", [P, T])
        ge = sb("ge", [P, T])
        gs = sb("gs", [P, T])
        g1 = sb("g1", [P, T])
        g2 = sb("g2", [P, T])
        gm1 = sb("gm1", [P, T, E])
        gm2 = sb("gm2", [P, T, E])
        gate = sb("gate", [P, T, E])
        g24 = sb("g24", [P, T, 3 * E], F32R)
        g24t = sb("g24t", [3 * E, HW], F32R)
        prod = [sb(f"prod_{p}", [P, E * C]) for p in range(2)]
        outc = sb("outc", [P, HW])

        ps_conv = psum("ps_conv")
        ps_sim = psum("ps_sim", HW)
        ps_att = psum("ps_att", HW)
        ps_ffn = psum("ps_ffn", E * C)
        ps_misc = psum("ps_misc")

        s_const = sem("s_const")
        s_wsplit = sem("s_wsplit")
        s_gnpad = sem("s_gnpad")
        s_nhalf = sem("s_nhalf")
        s_gstats = sem("s_gstats")
        s_gmv = sem("s_gmv")
        s_gmean_ps = sem("s_gmean_ps")
        s_gmeanv = sem("s_gmeanv")
        s_gvar_ps = sem("s_gvar_ps")
        s_gve = sem("s_gve")
        s_grs = sem("s_grs")
        s_gnf = sem("s_gnf")
        s_gnhi = sem("s_gnhi")
        s_gnlo = sem("s_gnlo")
        s_conv_ps = sem("s_conv_ps")
        s_x1c = sem("s_x1c")
        s_x1t_ps = sem("s_x1t_ps")
        s_x1t = sem("s_x1t")
        s_l1st = sem("s_l1st")
        s_l1mv = sem("s_l1mv")
        s_l1ve = sem("s_l1ve")
        s_l1rs = sem("s_l1rs")
        s_l1q = sem("s_l1q")
        s_l1n = sem("s_l1n")
        s_l1a = sem("s_l1a")
        s_xnt = sem("s_xnt")
        s_xn_ps = sem("s_xn_ps")
        s_xnhi = sem("s_xnhi")
        s_xnlo = sem("s_xnlo")
        s_sim_ps = sem("s_sim_ps")
        s_e_tile = sem("s_e_tile")
        s_rinv = sem("s_rinv")
        s_rb_ps = sem("s_rb_ps")
        s_rb = sem("s_rb")
        s_s_tile = sem("s_s_tile")
        s_f_tile = sem("s_f_tile")
        s_s_hi = sem("s_s_hi")
        s_s_lo = sem("s_s_lo")
        s_ci = sem("s_ci")
        s_key_step = sem("s_key_step")
        s_wlo = sem("s_wlo")
        s_h_tile = sem("s_h_tile")
        s_att_ps = sem("s_att_ps")
        s_u_tokens = sem("s_u_tokens")
        s_x1b = sem("s_x1b")
        s_ysum_ps = sem("s_ysum_ps")
        s_ysum = sem("s_ysum")
        s_xneg = sem("s_xneg")
        s_xnegt_ps = sem("s_xnegt_ps")
        s_yv = sem("s_yv")
        s_l2st = sem("s_l2st")
        s_l2mv = sem("s_l2mv")
        s_l2ve = sem("s_l2ve")
        s_l2rs = sem("s_l2rs")
        s_l2q = sem("s_l2q")
        s_t1 = sem("s_t1")
        s_l3st = sem("s_l3st")
        s_l3mv = sem("s_l3mv")
        s_l3ve = sem("s_l3ve")
        s_l3rs = sem("s_l3rs")
        s_z_tokens = sem("s_z_tokens")
        s_z_ps = sem("s_z_ps")
        s_zhi = sem("s_zhi")
        s_zlo = sem("s_zlo")
        s_logit_ps = sem("s_logit_ps")
        s_lg = sem("s_lg")
        s_mx = sem("s_mx")
        s_mi = sem("s_mi")
        s_gd = sem("s_gd")
        s_ge = sem("s_ge")
        s_gate = sem("s_gate")
        s_gate24 = sem("s_gate24")
        s_gt_ps = sem("s_gt_ps")
        s_gt = sem("s_gt")
        s_gb_ps = sem("s_gb_ps")
        s_t1b = sem("s_t1b")
        s_ffn_ps = sem("s_ffn_ps")
        s_prod = sem("s_prod")
        s_tree = sem("s_tree")
        s_t2 = sem("s_t2")
        s_out_ps = sem("s_out_ps")
        s_outc = sem("s_outc")
        s_stored = sem("s_stored")
        s_loaded = [sem(f"s_loaded{p}") for p in range(2)]

        block = ctx.enter_context(nc.Block())

        def half(ap, h):
            return ap[:, h * HALF:(h + 1) * HALF]

        def tile(ap, t):
            return ap[:, t * P:(t + 1) * P]

        def half_t(ap, h):
            return ap[:, h * TPH:(h + 1) * TPH, :]

        def padded(ap, h, dy=1, dx=1):
            return ap[:, h * RPH + dy:h * RPH + dy + RPH, dx:dx + W]

        def rows(ap):
            return ap.rearrange("p (r w) -> p r w", w=W)

        CONST_LOADS = 12
        WSPLIT = 10
        GMEAN, GATE, KEYS, TREE = 3, 10, 2, 3

        def count(value):
            return max(value, 0) if isinstance(value, int) else value

        def dram(ap, it, image):
            return ap[image.n] if it.static else ap[bass.ds(image.n, 1)].rearrange("a p n -> (a p) n")

        @block.sync
        def _(sp):
            es_flat = es[:].rearrange("p t n -> p (t n)")
            loads = [(ident[:], identity), (gmat[:], group_mean), (ids[:], expert_ids), (rows24[:], bias_rows),
                     (cb[:], conv_b), (lnw[:], ln_w), (lnb[:], ln_b), (rb[:], router_b), (eb[:], expert_b),
                     (rw[:], router_w), (es_flat[:, 0:TAPS * C], conv_w),
                     (es_flat[:, TAPS * C:TAPS * C + E * C], expert_w)]
            sp.dma_start(xc[0][:], x[0]).then_inc(s_loaded[0], 16)
            for dst, src in loads:
                sp.dma_start(dst, src).then_inc(s_const, 16)

            def run(it):
                a, o = it.image(2), it.image(-3)
                if a and not (it.static and a.n == 0):
                    sp.wait_ge(s_x1c, count(NH * (a.n - 2) + NH))
                    sp.dma_start(xc[a.par][:], dram(x, it, a)).then_inc(s_loaded[a.par], 16)
                if o:
                    sp.wait_ge(s_outc, NH * o.n + NH)
                    sp.dma_start(dram(out, it, o), outc[:]).then_inc(s_stored, 16)

            iterations(sp, NB, run)
            sp.wait_ge(s_stored, 16 * NB)

        @block.tensor
        def _(pe):
            pe.wait_ge(s_const, 16 * CONST_LOADS)
            pe.wait_ge(s_wsplit, WSPLIT)
            mm = nc.tensor.matmul
            PARTS = 3

            def run(it):
                a, b, c, v, w, o = (it.image(d) for d in (2, 1, 0, -1, -2, -3))

                if c:
                    reader = (s_xnlo, NH * c.n + NH)
                elif o:
                    reader = (s_t1b, NH * o.n + NH)
                elif b:
                    reader = (s_gve, b.n + 1)
                else:
                    reader = (s_gve, 0)

                def sim(t):
                    pe.wait_ge(s_xnlo, NH * c.n + NH)
                    pe.wait_ge(s_e_tile, T * c.n + t)
                    hi, lo = xnhi[c.par], xnlo[c.par]
                    for h in range(NH):
                        mm(half(ps_sim, h), tile(hi, t), half(hi, h), start=True, stop=False)
                        mm(half(ps_sim, h), tile(hi, t), half(lo, h), start=False, stop=False)
                        m = mm(half(ps_sim, h), tile(lo, t), half(hi, h), start=False, stop=True)
                    m.then_inc(s_sim_ps, 1)

                conv_done = 0

                def conv(count):
                    nonlocal conv_done
                    for k in range(conv_done, conv_done + count):
                        h, n = divmod(k, TAPS * PARTS)
                        tap, part = divmod(n, PARTS)
                        if n == 0:
                            pe.wait_ge(s_gnhi, b.n + 1)
                            pe.wait_ge(s_gnlo, b.n + 1)
                            pe.wait_ge(s_x1c, NH * b.n + h)
                        wts, src = ((cwhi, gnhi), (cwhi, gnlo), (cwlo, gnhi))[part]
                        m = mm(rows(ps_conv[:]), wts[:, tap, :], padded(src, h, tap // KS, tap % KS),
                               start=(n == 0), stop=(n == TAPS * PARTS - 1))
                        if n == TAPS * PARTS - 1:
                            m.then_inc(s_conv_ps, 1)
                    conv_done += count

                def attend(g, k):
                    pe.wait_ge(s_s_hi, T * g.n + k + 1)
                    pe.wait_ge(s_s_lo, T * g.n + k + 1)
                    pe.wait_ge(s_wlo, T * g.n + k + 1)
                    pe.wait_ge(s_h_tile, T * g.n + k + 1)
                    if k == 0:
                        pe.wait_ge(s_xneg, NH * g.n)
                    r = k % 2
                    for h in range(NH):
                        mm(half(ps_att, h), whi[r][:], half(s1hi[r], h), start=(k == 0), stop=False)
                        mm(half(ps_att, h), whi[r][:], half(s1lo[r], h), start=False, stop=False)
                        mm(half(ps_att, h), wlo[r][:], half(s1hi[r], h), start=False, stop=False)
                        m = mm(half(ps_att, h), yhi[r][:], half(hx[r], h), start=False, stop=(k == T - 1))
                    m.then_inc(s_att_ps, 1)

                def ffn(t):
                    pe.wait_ge(s_zlo, NH * w.n + NH)
                    pe.wait_ge(s_prod, T * w.n + t)
                    for h in range(NH):
                        mm(half(ps_ffn, h), tile(zhi, t), half(ewhi, h), start=True, stop=False)
                        mm(half(ps_ffn, h), tile(zhi, t), half(ewlo, h), start=False, stop=False)
                        m = mm(half(ps_ffn, h), tile(zlo, t), half(ewhi, h), start=False, stop=True)
                    m.then_inc(s_ffn_ps, 1)

                def transposes(src_tile, h):
                    for q in range(TPH):
                        m = nc.tensor.transpose(tile(ps_misc, q), src_tile(h * TPH + q), ident[:])
                    return m

                def misc_rb(h):
                    nonlocal reader
                    pe.wait_ge(s_rinv, v.n + 1)
                    pe.wait_ge(*reader)
                    reader = (s_rb, NH * v.n + h + 1)
                    transposes(lambda t: rinv[:, t:t + 1].to_broadcast([P, P]), h).then_inc(s_rb_ps, 1)

                def misc_ysum():
                    nonlocal reader
                    pe.wait_ge(s_ci, T * w.n + T)
                    pe.wait_ge(*reader)
                    reader = (s_ysum, w.n + 1)
                    for t in range(T):
                        m = mm(ps_misc[:, 0:1], u[w.par][:, t, :], ci[w.par][:, t:t + 1],
                               start=(t == 0), stop=(t == T - 1))
                    m.then_inc(s_ysum_ps, 1)

                def misc_out(h):
                    nonlocal reader
                    pe.wait_ge(s_t2, T * o.n + T)
                    pe.wait_ge(*reader)
                    reader = (s_outc, NH * o.n + h + 1)
                    transposes(lambda t: t1[:, t, :], h).then_inc(s_out_ps, 1)

                def misc_xneg(h):
                    nonlocal reader
                    pe.wait_ge(s_xneg, NH * w.n + h + 1)
                    pe.wait_ge(*reader)
                    reader = (s_yv, NH * w.n + h + 1)
                    transposes(lambda t: tile(xneg, t), h).then_inc(s_xnegt_ps, 1)

                def misc_z(h):
                    nonlocal reader
                    pe.wait_ge(s_z_tokens, NH * w.n + h + 1)
                    pe.wait_ge(*reader)
                    reader = (s_zlo, NH * w.n + h + 1)
                    transposes(lambda t: zt[:, t, :], h).then_inc(s_z_ps, 1)

                def misc_router():
                    nonlocal reader
                    pe.wait_ge(s_zlo, NH * w.n + NH)
                    pe.wait_ge(*reader)
                    reader = (s_lg, w.n + 1)
                    for t in range(T):
                        dst = ps_misc[:, t * E:(t + 1) * E]
                        mm(dst, tile(zhi, t), rwhi[:], start=True, stop=False)
                        mm(dst, tile(zhi, t), rwlo[:], start=False, stop=False)
                        m = mm(dst, tile(zlo, t), rwhi[:], start=False, stop=True)
                    m.then_inc(s_logit_ps, 1)

                def misc_gmean():
                    nonlocal reader
                    pe.wait_ge(s_gmv, a.n + 1)
                    pe.wait_ge(*reader)
                    reader = (s_gmeanv, GMEAN * a.n + 1)
                    mm(ps_misc[:, 0:1], gmat[:], gmv[:, 0:1], start=True, stop=True).then_inc(s_gmean_ps, 1)

                def misc_gvar():
                    nonlocal reader
                    pe.wait_ge(s_gmeanv, GMEAN * a.n + GMEAN)
                    pe.wait_ge(*reader)
                    reader = (s_gve, a.n + 1)
                    mm(ps_misc[:, 0:1], gmat[:], gv[:], start=True, stop=True).then_inc(s_gvar_ps, 1)

                def misc_x1(h):
                    nonlocal reader
                    pe.wait_ge(s_x1c, NH * b.n + h + 1)
                    pe.wait_ge(*reader)
                    reader = (s_x1t, NH * b.n + h + 1)
                    transposes(lambda t: tile(x1c, t), h).then_inc(s_x1t_ps, 1)

                def misc_gt(h):
                    nonlocal reader
                    pe.wait_ge(s_gate24, w.n + 1)
                    pe.wait_ge(*reader)
                    reader = (s_gt, NH * w.n + h + 1)
                    for q in range(TPH):
                        m = nc.tensor.transpose(ps_misc[0:3 * E, q * P:(q + 1) * P],
                                                g24[:, h * TPH + q, :].bitcast(F32), ident[:])
                    m.then_inc(s_gt_ps, 1)

                def misc_gb(h):
                    nonlocal reader
                    pe.wait_ge(s_gt, NH * w.n + h + 1)
                    pe.wait_ge(*reader)
                    reader = (s_t1b, NH * w.n + h + 1)
                    for q in range(TPH):
                        m = mm(tile(ps_misc, q), tile(g24t, h * TPH + q), ebs[:], start=True, stop=True)
                    m.then_inc(s_gb_ps, 1)

                def misc_xn(h):
                    nonlocal reader
                    pe.wait_ge(s_xnt, NH * b.n + h + 1)
                    pe.wait_ge(*reader)
                    reader = (s_xnlo, NH * b.n + h + 1)
                    transposes(lambda t: xnt[:, t, :], h).then_inc(s_xn_ps, 1)

                if v:
                    misc_rb(0)
                if c:
                    sim(0)
                if b:
                    conv(CONV_MM[0][0])
                if v:
                    misc_rb(1)
                if b:
                    conv(CONV_MM[0][1])
                if w:
                    attend(w, T - 1)
                    misc_ysum()
                if o:
                    misc_out(0)
                if c:
                    sim(1)
                if b:
                    conv(CONV_MM[1][0])
                if o:
                    misc_out(1)
                if b:
                    conv(CONV_MM[1][1])
                if w:
                    misc_xneg(0)
                if v:
                    attend(v, 0)
                if w:
                    misc_xneg(1)
                if c:
                    sim(2)
                if b:
                    conv(sum(CONV_MM[2]))
                    misc_x1(0)
                if v:
                    attend(v, 1)
                if c:
                    sim(3)
                if b:
                    conv(CONV_MM[3][0])
                if w:
                    misc_z(0)
                if b:
                    conv(CONV_MM[3][1])
                if w:
                    misc_z(1)
                if v:
                    attend(v, 2)
                if w:
                    misc_router()
                if a:
                    misc_gmean()
                if c:
                    sim(4)
                if b:
                    misc_x1(1)
                if w:
                    ffn(0)
                if v:
                    attend(v, 3)
                if w:
                    misc_gt(0)
                if a:
                    misc_gvar()
                if w:
                    misc_gt(1)
                if c:
                    sim(5)
                if w:
                    ffn(1)
                    misc_gb(0)
                if v:
                    attend(v, 4)
                if w:
                    misc_gb(1)
                    ffn(2)
                if c:
                    sim(6)
                if w:
                    ffn(3)
                if v:
                    attend(v, 5)
                if w:
                    ffn(4)
                if c:
                    sim(7)
                if w:
                    ffn(5)
                if b:
                    misc_xn(0)
                if v:
                    attend(v, 6)
                if w:
                    ffn(6)
                if b:
                    misc_xn(1)
                if w:
                    ffn(7)

            iterations(pe, NB, run)

        @block.scalar
        def _(act):
            act.wait_ge(s_gnpad, 2)
            act.wait_ge(s_wsplit, WSPLIT)

            def run(it):
                a, b, c, v, w, o = (it.image(d) for d in (2, 1, 0, -1, -2, -3))

                def exp_sim(t):
                    act.wait_ge(s_sim_ps, T * c.n + t + 1)
                    if v:
                        act.wait_ge(s_s_tile, T * v.n + t + 1)
                    nc.scalar.activation(es[:, t, :], ps_sim[:], ACT.Exp, scale=INV_TEMP,
                                         accum_out=rsum[c.par][:, t:t + 1]).then_inc(s_e_tile, 1)

                def exp_s(t):
                    act.wait_ge(s_s_tile, T * v.n + t + 1)
                    act.wait_ge(s_h_tile, count(T * v.n + t - 1))
                    nc.scalar.activation(fx[t % 2][:], s1[t % 2][:], ACT.Exp,
                                         accum_out=csum[v.par][:, t:t + 1]).then_inc(s_f_tile, 1)

                def round_s(t):
                    act.wait_ge(s_att_ps, count(T * v.n + t - 1))
                    nc.scalar.copy(s1hi[t % 2][:], s1[t % 2][:]).then_inc(s_s_hi, 1)

                def rb_copy(h):
                    act.wait_ge(s_rb_ps, NH * v.n + h + 1)
                    act.wait_ge(s_s_tile, T * v.n)
                    nc.scalar.copy(half(rbc, h), ps_misc[:]).then_inc(s_rb, 1)

                def xneg_copy(h):
                    act.wait_ge(s_ysum, w.n + 1)
                    act.wait_ge(s_att_ps, T * w.n + T)
                    act.wait_ge(s_xnegt_ps, NH * w.n)
                    nc.scalar.activation(half(xneg, h), half(ps_att, h), ACT.Identity,
                                         bias=ysum[:]).then_inc(s_xneg, 1)

                def out_copy(h):
                    act.wait_ge(s_out_ps, NH * o.n + h + 1)
                    act.wait_ge(s_stored, 16 * o.n)
                    nc.scalar.copy(half(outc, h), ps_misc[:]).then_inc(s_outc, 1)

                def x1_copy(h):
                    act.wait_ge(s_x1t_ps, NH * b.n + h + 1)
                    act.wait_ge(s_x1b, count(b.n - 1))
                    act.wait_ge(s_u_tokens, count(b.n - 1))
                    nc.scalar.copy(half(x1t[b.par][:].rearrange("p t c -> p (t c)"), h), ps_misc[:]).then_inc(s_x1t, 1)

                def z_round(h):
                    act.wait_ge(s_z_ps, NH * w.n + h + 1)
                    act.wait_ge(s_ffn_ps, T * w.n)
                    nc.scalar.copy(half(zhi, h), ps_misc[:]).then_inc(s_zhi, 1)

                def gate_copy(h):
                    act.wait_ge(s_gt_ps, NH * w.n + h + 1)
                    act.wait_ge(s_gb_ps, NH * w.n)
                    nc.scalar.copy(half(g24t, h), ps_misc[0:3 * E, :]).then_inc(s_gt, 1)

                def xn_round(h):
                    act.wait_ge(s_xn_ps, NH * b.n + h + 1)
                    act.wait_ge(s_sim_ps, count(T * (b.n - 1)))
                    nc.scalar.copy(half(xnhi[b.par], h), ps_misc[:]).then_inc(s_xnhi, 1)

                for s in range(T):
                    if s == 0 and v:
                        rb_copy(0)
                        rb_copy(1)
                    if s == 1 and w:
                        xneg_copy(0)
                        xneg_copy(1)
                    if s == 4 and w:
                        act.wait_ge(s_gd, w.n + 1)
                        nc.scalar.activation(ge[:], gd[:], ACT.Exp).then_inc(s_ge, 1)
                    if c:
                        exp_sim(s)
                    if s == 1 and o:
                        out_copy(0)
                    if s == 4 and b:
                        x1_copy(1)
                    if s == 7 and b:
                        xn_round(0)
                    if v:
                        exp_s(s)
                    if s == 1 and o:
                        out_copy(1)
                    if s == 3 and w:
                        z_round(0)
                    if v:
                        round_s(s)
                    if s == 2 and b:
                        x1_copy(0)
                    if s == 3 and w:
                        z_round(1)
                    if s == 4 and w:
                        gate_copy(0)
                        gate_copy(1)
                    if s == 6 and a:
                        act.wait_ge(s_gnf, a.n + 1)
                        if b:
                            act.wait_ge(s_conv_ps, NH * b.n + NH)
                        nc.scalar.copy(gnhi[:, 1:1 + H, 1:1 + W], rows(gnf)).then_inc(s_gnhi, 1)
                    if s == 7 and b:
                        xn_round(1)

            iterations(act, NB, run)

        @block.gpsimd
        def _(pool):
            add = nc.gpsimd.tensor_tensor
            nc.gpsimd.memset(nhalf[:], -0.5).then_inc(s_nhalf, 1)
            nc.gpsimd.memset(gnhi[:].bitcast(F32), 0.0).then_inc(s_gnpad, 1)
            nc.gpsimd.memset(gnlo[:].bitcast(F32), 0.0).then_inc(s_gnpad, 1)
            pool.wait_ge(s_nhalf, 1)
            pool.wait_ge(s_const, 16 * CONST_LOADS)

            def run(it):
                a, b, c, v, w, o = (it.image(d) for d in (2, 1, 0, -1, -2, -3))

                def inv_sqrt(dst, src):
                    return nc.gpsimd.tensor_tensor(dst, src, nhalf[:].to_broadcast([P, src.shape[1]]), ALU.pow)

                def low_s(t):
                    pool.wait_ge(s_s_hi, T * v.n + t + 1)
                    pool.wait_ge(s_att_ps, count(T * v.n + t - 1))
                    nc.gpsimd.tensor_tensor(s1lo[t % 2][:], s1[t % 2][:], s1hi[t % 2][:].bitcast(F32),
                                            ALU.subtract).then_inc(s_s_lo, 1)

                def expert_sum(t):
                    p = prod[t % 2]
                    pool.wait_ge(s_prod, T * w.n + t + 1)
                    for k in range(TREE):
                        n = E * C >> (k + 1)
                        add(p[:, 0:n], p[:, 0:n], p[:, n:2 * n], ALU.add).then_inc(s_tree, 1)
                        pool.wait_ge(s_tree, TREE * (T * w.n + t) + k + 1)
                    pool.wait_ge(s_t1b, NH * w.n + NH)
                    add(t1[:, t, :], t1[:, t, :], p[:, 0:C], ALU.add).then_inc(s_t2, 1)

                for s in range(T):
                    if s == 1 and w:
                        pool.wait_ge(s_l2ve, w.n + 1)
                        inv_sqrt(l2rs[:], l2ve[:]).then_inc(s_l2rs, 1)
                    if s == 2 and w:
                        pool.wait_ge(s_l3ve, w.n + 1)
                        inv_sqrt(l3rs[:], l3ve[:]).then_inc(s_l3rs, 1)
                    if s == 5 and b:
                        pool.wait_ge(s_l1ve, b.n + 1)
                        pool.wait_ge(s_u_tokens, count(b.n - 1))
                        inv_sqrt(l1rs[b.par][:], l1ve[:]).then_inc(s_l1rs, 1)
                        pool.wait_ge(s_l1q, 3 * b.n + 3)
                        inv_sqrt(l1in[:], l1n[:]).then_inc(s_l1n, 1)
                    if s == 5 and a:
                        pool.wait_ge(s_gve, a.n + 1)
                        inv_sqrt(grs[:], gve[:]).then_inc(s_grs, 1)
                    if v:
                        low_s(s)
                    if s == 0 and v:
                        pool.wait_ge(s_x1t, NH * v.n + NH)
                        pool.wait_ge(s_t1, count(NH * (v.n - 2) + NH))
                        nc.gpsimd.tensor_tensor(x1b[v.par][:], x1t[v.par][:], lnb[:].unsqueeze(1).to_broadcast([P, T, C]),
                                                ALU.add).then_inc(s_x1b, 1)
                    if w:
                        for t in ((), (), (), (), (), (0, 1, 2), (3, 4), (5, 6, 7))[s]:
                            expert_sum(t)

            iterations(pool, NB, run)

        @block.vector
        def _(dve):
            V = nc.vector
            es_flat = es[:].rearrange("p t n -> p (t n)")
            dve.wait_ge(s_const, 16 * CONST_LOADS)
            cw = es_flat[:, 0:TAPS * C]
            ew = es_flat[:, TAPS * C:TAPS * C + E * C]
            cwh, cwl = (q[:].rearrange("p a b -> p (a b)") for q in (cwhi, cwlo))
            V.tensor_copy(cwh, cw).then_inc(s_wsplit, 1)
            V.tensor_copy(ewhi[:], ew).then_inc(s_wsplit, 1)
            V.tensor_copy(rwhi[:], rw[:]).then_inc(s_wsplit, 1)
            V.tensor_copy(ebhi[:], eb[:]).then_inc(s_wsplit, 1)
            dve.wait_ge(s_wsplit, 4)
            V.tensor_tensor(cwl, cw, cwh.bitcast(F32), ALU.subtract).then_inc(s_wsplit, 1)
            V.tensor_tensor(ewlo[:], ew, ewhi[:].bitcast(F32), ALU.subtract).then_inc(s_wsplit, 1)
            V.tensor_tensor(rwlo[:], rw[:], rwhi[:].bitcast(F32), ALU.subtract).then_inc(s_wsplit, 1)
            V.tensor_tensor(eblo[:], eb[:], ebhi[:].bitcast(F32), ALU.subtract).then_inc(s_wsplit, 1)
            dve.wait_ge(s_wsplit, 8)
            V.tensor_scalar(ebt[:], eblo[:], rows24[:, 1:2], None, ALU.mult).then_inc(s_wsplit, 1)
            dve.wait_ge(s_wsplit, 9)
            V.scalar_tensor_tensor(out=ebs[:], in0=ebhi[:].bitcast(F32), scalar=rows24[:, 0:1], in1=ebt[:],
                                   op0=ALU.mult, op1=ALU.add).then_inc(s_wsplit, 1)

            def run(it):
                a, b, c, v, w, o = (it.image(d) for d in (2, 1, 0, -1, -2, -3))

                def flat(ap, h):
                    return half_t(ap, h).rearrange("p t c -> p (t c)")

                def of_half(h):
                    return range(h * TPH, (h + 1) * TPH)

                def token_stats(src, st, mv, h, g, st_done, mv_done):
                    for t in of_half(h):
                        i_ = V.bn_stats(st[:, t, :], src[:, t, :])
                    i_.then_inc(st_done, 1)
                    dve.wait_ge(s_wsplit, 1)
                    dve.wait_ge(st_done, NH * g.n + h + 1)
                    for t in of_half(h):
                        i_ = V.bn_aggr(mv[:, t, :], st[:, t, :])
                    i_.then_inc(mv_done, 1)

                def scale_rows(k):
                    dve.wait_ge(s_rb, NH * v.n + NH)
                    dve.wait_ge(s_s_lo, count(T * v.n + k - 1))
                    dve.wait_ge(s_f_tile, count(T * v.n + k - 1))
                    dve.wait_ge(s_h_tile, count(T * v.n + k - 1))
                    V.tensor_tensor(s1[k % 2][:], es[:, k, :], rbc[:], ALU.mult).then_inc(s_s_tile, 1)

                def keys(g, k):
                    p, r = g.par, k % 2
                    n = T * g.n + k
                    dve.wait_ge(s_f_tile, n + 1)
                    cik = ci[p][:, k:k + 1]
                    V.reciprocal(cik, csum[p][:, k:k + 1]).then_inc(s_ci, 1)
                    dve.wait_ge(s_att_ps, count(n - 1))
                    dve.wait_ge(s_wlo, n)
                    V.scalar_tensor_tensor(out=hx[r][:], in0=fx[r][:], scalar=-1.0, in1=s1[r][:],
                                           op0=ALU.add, op1=ALU.subtract).then_inc(s_h_tile, 1)
                    dve.wait_ge(s_ci, n + 1)
                    V.tensor_scalar(ci1[:, k:k + 1], cik, 1.0, None, ALU.add).then_inc(s_key_step, 1)
                    V.tensor_scalar(yhi[r][:], u[p][:, k, :], cik, None, ALU.mult)
                    dve.wait_ge(s_key_step, KEYS * n + 1)
                    V.tensor_scalar(whi[r][:], u[p][:, k, :], ci1[:, k:k + 1], None, ALU.mult)
                    V.tensor_scalar(wf[:], u[p][:, k, :], ci1[:, k:k + 1], None, ALU.mult).then_inc(s_key_step, 1)
                    dve.wait_ge(s_key_step, KEYS * n + 2)
                    V.tensor_tensor(wlo[r][:], wf[:], whi[r][:].bitcast(F32), ALU.subtract).then_inc(s_wlo, 1)

                def unit_tokens():
                    dve.wait_ge(s_l1rs, v.n + 1)
                    dve.wait_ge(s_yv, count(NH * (v.n - 2) + NH))
                    dve.wait_ge(s_ysum_ps, count(v.n - 1))
                    for t in range(T):
                        i_ = V.tensor_scalar(u[v.par][:, t, :], x1t[v.par][:, t, :], l1mv[v.par][:, t, 0:1],
                                             l1rs[v.par][:, t:t + 1], ALU.subtract, ALU.mult)
                    i_.then_inc(s_u_tokens, 1)
                    dve.wait_ge(s_u_tokens, v.n + 1)

                def residual_norm():
                    dve.wait_ge(s_l2rs, w.n + 1)
                    dve.wait_ge(s_x1b, w.n + 1)
                    if o:
                        dve.wait_ge(s_out_ps, NH * o.n + NH)
                    for h in range(NH):
                        for t in of_half(h):
                            i_ = V.scalar_tensor_tensor(out=yv[:, t, :], in0=yv[:, t, :], scalar=l2mv[:, t, 0:1],
                                                        in1=lnw[:], op0=ALU.subtract, op1=ALU.mult)
                        i_.then_inc(s_l2q, 1)
                        dve.wait_ge(s_l2q, NH * w.n + h + 1)
                        for t in of_half(h):
                            i_ = V.scalar_tensor_tensor(out=t1[:, t, :], in0=yv[:, t, :], scalar=l2rs[:, t:t + 1],
                                                        in1=x1b[w.par][:, t, :], op0=ALU.mult, op1=ALU.add)
                        i_.then_inc(s_t1, 1)
                        dve.wait_ge(s_t1, NH * w.n + h + 1)
                        token_stats(t1, l3st, l3mv, h, w, s_l3st, s_l3mv)
                    dve.wait_ge(s_l3mv, NH * w.n + NH)
                    V.tensor_scalar(l3ve[:], l3mv[:, :, 1], LNT_EPS, None, ALU.add).then_inc(s_l3ve, 1)

                def two_largest():
                    dve.wait_ge(s_wsplit, 1)
                    dve.wait_ge(s_lg, w.n + 1)
                    for t in range(T):
                        i_ = V.max(mx[:, t, :], lg[:, t, :])
                    i_.then_inc(s_mx, 1)
                    dve.wait_ge(s_mx, w.n + 1)
                    V.tensor_tensor(gd[:], mx[:, :, 1], mx[:, :, 0], ALU.subtract).then_inc(s_gd, 1)
                    for t in range(T):
                        i_ = V.max_index(mi[:, t, :], mx[:, t, :], lg[:, t, :])
                    i_.then_inc(s_mi, 1)
                    dve.wait_ge(s_mi, NH * w.n + 1)
                    V.tensor_copy(mf[:].rearrange("p k t -> p t k"), mi[:, :, 0:2]).then_inc(s_mi, 1)

                def gates():
                    def wide(ap):
                        return ap.unsqueeze(2).to_broadcast([P, T, E])

                    g0 = GATE * w.n
                    dve.wait_ge(s_mi, 2 * w.n + 2)
                    V.tensor_tensor(gm1[:], ids[:], wide(mf[:, 0, :]), ALU.is_equal).then_inc(s_gate, 1)
                    V.tensor_tensor(gm2[:], ids[:], wide(mf[:, 1, :]), ALU.is_equal).then_inc(s_gate, 1)
                    dve.wait_ge(s_ge, w.n + 1)
                    V.tensor_scalar(gs[:], ge[:], 1.0, None, ALU.add).then_inc(s_gate, 1)
                    dve.wait_ge(s_gate, g0 + 3)
                    V.reciprocal(g1[:], gs[:]).then_inc(s_gate, 1)
                    dve.wait_ge(s_gate, g0 + 4)
                    V.tensor_tensor(g2[:], ge[:], g1[:], ALU.mult).then_inc(s_gate, 1)
                    V.tensor_tensor(gm1[:], gm1[:], wide(g1[:]), ALU.mult).then_inc(s_gate, 1)
                    dve.wait_ge(s_gate, g0 + 6)
                    V.tensor_tensor(gm2[:], gm2[:], wide(g2[:]), ALU.mult).then_inc(s_gate, 1)
                    dve.wait_ge(s_gate, g0 + 7)
                    V.tensor_tensor(gate[:], gm1[:], gm2[:], ALU.add).then_inc(s_gate, 1)
                    dve.wait_ge(s_gate, g0 + 8)
                    dve.wait_ge(s_gt_ps, NH * w.n)
                    V.tensor_copy(g24[:, :, 0:E], gate[:]).then_inc(s_gate, 1)
                    V.tensor_copy(g24[:, :, 2 * E:3 * E], gate[:]).then_inc(s_gate, 1)
                    dve.wait_ge(s_gate, g0 + 9)
                    V.tensor_tensor(g24[:, :, E:2 * E], gate[:], g24[:, :, 0:E].bitcast(F32),
                                    ALU.subtract).then_inc(s_gate24, 1)

                def gated_bias(h):
                    dve.wait_ge(s_gb_ps, NH * w.n + h + 1)
                    V.tensor_tensor(flat(t1, h), flat(t1, h), ps_misc[:], ALU.add).then_inc(s_t1b, 1)

                def gate_experts(t):
                    dve.wait_ge(s_gate, GATE * w.n + 8)
                    dve.wait_ge(s_ffn_ps, T * w.n + t + 1)
                    dve.wait_ge(s_t2, count(T * w.n + t - 1))
                    V.tensor_tensor(prod[t % 2][:].rearrange("p (e c) -> p e c", e=E),
                                    ps_ffn[:].rearrange("p (e c) -> p e c", e=E),
                                    gate[:, t, :].unsqueeze(2).to_broadcast([P, E, C]),
                                    ALU.mult).then_inc(s_prod, 1)

                def conv_out(h):
                    dve.wait_ge(s_conv_ps, NH * b.n + h + 1)
                    dve.wait_ge(s_x1t_ps, NH * b.n)
                    dve.wait_ge(s_loaded[b.par], 16 * b.nth + 16)
                    V.scalar_tensor_tensor(out=half(x1c, h), in0=ps_conv[:], scalar=cb[:], in1=half(xc[b.par], h),
                                           op0=ALU.add, op1=ALU.add).then_inc(s_x1c, 1)

                def first_stats(h):
                    dve.wait_ge(s_x1t, NH * b.n + h + 1)
                    token_stats(x1t[b.par], l1st, l1mv[b.par], h, b, s_l1st, s_l1mv)

                def first_norms():
                    dve.wait_ge(s_l1mv, NH * b.n + NH)
                    V.tensor_scalar(l1ve[:], l1mv[b.par][:, :, 1], LNT_EPS, None, ALU.add).then_inc(s_l1ve, 1)
                    dve.wait_ge(s_l1ve, b.n + 1)
                    V.reciprocal(l1rec[:], l1ve[:]).then_inc(s_l1q, 1)
                    dve.wait_ge(s_l1q, 3 * b.n + 1)
                    V.scalar_tensor_tensor(out=l1q[:], in0=l1rec[:], scalar=float(C), in1=l1mv[b.par][:, :, 1],
                                           op0=ALU.mult, op1=ALU.mult).then_inc(s_l1q, 1)
                    dve.wait_ge(s_l1q, 3 * b.n + 2)
                    V.tensor_scalar(l1n[:], l1q[:], 1e-24, None, ALU.max).then_inc(s_l1q, 1)

                def normalise():
                    dve.wait_ge(s_l1rs, b.n + 1)
                    dve.wait_ge(s_l1n, b.n + 1)
                    V.tensor_tensor(l1a[:], l1rs[b.par][:], l1in[:], ALU.mult).then_inc(s_l1a, 1)
                    dve.wait_ge(s_l1a, b.n + 1)
                    if w:
                        dve.wait_ge(s_z_ps, NH * w.n + NH)
                    dve.wait_ge(s_xn_ps, NH * b.n)
                    for h in range(NH):
                        for t in of_half(h):
                            i_ = V.tensor_scalar(xnt[:, t, :], x1t[b.par][:, t, :], l1mv[b.par][:, t, 0:1],
                                                 l1a[:, t:t + 1], ALU.subtract, ALU.mult)
                        i_.then_inc(s_xnt, 1)

                def low_xn(h):
                    dve.wait_ge(s_xnhi, NH * b.n + h + 1)
                    V.tensor_tensor(half(xnlo[b.par], h), ps_misc[:], half(xnhi[b.par], h).bitcast(F32),
                                    ALU.subtract).then_inc(s_xnlo, 1)

                if v:
                    dve.wait_ge(s_e_tile, T * v.n + T)
                    dve.wait_ge(s_rb_ps, NH * v.n)
                    V.reciprocal(rinv[:], rsum[v.par][:]).then_inc(s_rinv, 1)
                if w:
                    keys(w, T - 1)
                if v:
                    scale_rows(0)
                    scale_rows(1)
                    unit_tokens()
                if w:
                    dve.wait_ge(s_ysum_ps, w.n + 1)
                    dve.wait_ge(s_xneg, NH * w.n)
                    V.tensor_copy(ysum[:], ps_misc[:, 0:1]).then_inc(s_ysum, 1)
                if v:
                    keys(v, 0)
                    scale_rows(2)
                if b:
                    conv_out(0)
                if w:
                    for h in range(NH):
                        dve.wait_ge(s_xnegt_ps, NH * w.n + h + 1)
                        V.scalar_tensor_tensor(out=flat(yv, h), in0=ps_misc[:], scalar=-SCALE,
                                               in1=flat(u[w.par], h), op0=ALU.mult, op1=ALU.add).then_inc(s_yv, 1)
                        dve.wait_ge(s_yv, NH * w.n + h + 1)
                        token_stats(yv, l2st, l2mv, h, w, s_l2st, s_l2mv)
                    dve.wait_ge(s_l2mv, NH * w.n + NH)
                    V.tensor_scalar(l2ve[:], l2mv[:, :, 1], ATTN_EPS, None, ALU.add).then_inc(s_l2ve, 1)
                if v:
                    keys(v, 1)
                    scale_rows(3)
                if w:
                    residual_norm()
                if a:
                    dve.wait_ge(s_loaded[a.par], 16 * a.nth + 16)
                    for h in range(NH):
                        i_ = V.bn_stats(gst[:, h, :], half(xc[a.par], h))
                    i_.then_inc(s_gstats, 1)
                if a:
                    dve.wait_ge(s_gstats, a.n + 1)
                if v:
                    keys(v, 2)
                    scale_rows(4)
                if a:
                    V.bn_aggr(gmv[:], gst[:].rearrange("p a b -> p (a b)")).then_inc(s_gmv, 1)
                if w:
                    dve.wait_ge(s_l3rs, w.n + 1)
                    if c:
                        dve.wait_ge(s_xn_ps, NH * c.n + NH)
                    for h in range(NH):
                        for t in of_half(h):
                            i_ = V.tensor_scalar(zt[:, t, :], t1[:, t, :], l3mv[:, t, 0:1], l3rs[:, t:t + 1],
                                                 ALU.subtract, ALU.mult)
                        i_.then_inc(s_z_tokens, 1)
                    for h in range(NH):
                        dve.wait_ge(s_zhi, NH * w.n + h + 1)
                        V.tensor_tensor(half(zlo, h), ps_misc[:], half(zhi, h).bitcast(F32),
                                        ALU.subtract).then_inc(s_zlo, 1)
                if b:
                    first_stats(0)
                if w:
                    dve.wait_ge(s_logit_ps, w.n + 1)
                    V.tensor_tensor(lg[:], ps_misc[:, 0:T * E].rearrange("p (t e) -> p t e", e=E), rb[:],
                                    ALU.add).then_inc(s_lg, 1)
                if a:
                    dve.wait_ge(s_gmean_ps, a.n + 1)
                    V.tensor_copy(gmean[:], ps_misc[:, 0:1]).then_inc(s_gmeanv, 1)
                    dve.wait_ge(s_gmeanv, GMEAN * a.n + 1)
                    V.tensor_tensor(gdev[:], gmv[:, 0:1], gmean[:], ALU.subtract).then_inc(s_gmeanv, 1)
                    dve.wait_ge(s_gmeanv, GMEAN * a.n + 2)
                    V.scalar_tensor_tensor(out=gv[:], in0=gdev[:], scalar=gdev[:], in1=gmv[:, 1:2],
                                           op0=ALU.mult, op1=ALU.add).then_inc(s_gmeanv, 1)
                if w:
                    two_largest()
                if b:
                    conv_out(1)
                if v:
                    keys(v, 3)
                if w:
                    gates()
                if v:
                    scale_rows(5)
                if a:
                    dve.wait_ge(s_gvar_ps, a.n + 1)
                    V.tensor_scalar(gve[:], ps_misc[:, 0:1], GN_EPS, None, ALU.add).then_inc(s_gve, 1)
                if w:
                    gate_experts(0)
                if v:
                    keys(v, 4)
                if w:
                    gated_bias(0)
                    gate_experts(1)
                if v:
                    scale_rows(6)
                if w:
                    gated_bias(1)
                if b:
                    first_stats(1)
                    first_norms()
                if w:
                    gate_experts(2)
                if v:
                    keys(v, 5)
                if w:
                    gate_experts(3)
                if v:
                    scale_rows(7)
                if a:
                    dve.wait_ge(s_grs, a.n + 1)
                    V.tensor_scalar(gnf, xc[a.par][:], gmean[:], grs[:], ALU.subtract, ALU.mult).then_inc(s_gnf, 1)
                if b:
                    normalise()
                if w:
                    gate_experts(4)
                if v:
                    keys(v, 6)
                if w:
                    gate_experts(5)
                if b:
                    low_xn(0)
                if w:
                    gate_experts(6)
                if b:
                    low_xn(1)
                if a:
                    dve.wait_ge(s_gnhi, a.n + 1)
                    V.tensor_tensor(gnlo[:, 1:1 + H, 1:1 + W], rows(gnf),
                                    gnhi[:, 1:1 + H, 1:1 + W].bitcast(F32), ALU.subtract).then_inc(s_gnlo, 1)
                if w:
                    gate_experts(7)

            iterations(dve, NB, run)


def kernel(x, L0_conv_weight, L0_conv_bias, L1_attn_ln_weight, L1_attn_ln_bias,
           L1_ffn_router_w, L1_ffn_router_b, L1_ffn_expert_w, L1_ffn_expert_b):
    import numpy as np
    import concourse.bacc as bacc
    from concourse.bass_utils import run_bass_kernel_spmd

    x = np.asarray(x)
    nb, c, h, w = x.shape
    tiles = h * w // P
    experts = L1_ffn_expert_b.shape[0]
    conv_weight, expert_weight = np.asarray(L0_conv_weight), np.asarray(L1_ffn_expert_w)
    group = c // 32
    same_group = np.arange(c)[:, None] // group == np.arange(c)[None, :] // group
    bias_rows = np.zeros((3 * experts, 2), np.float32)
    bias_rows[:2 * experts, 0] = 1
    bias_rows[2 * experts:, 1] = 1
    arrays = {
        "x": x.reshape(nb, c, h * w),
        "conv_w": conv_weight.transpose(1, 2, 3, 0).reshape(c, -1),
        "conv_b": np.asarray(L0_conv_bias).reshape(c, 1),
        "ln_w": np.broadcast_to(np.asarray(L1_attn_ln_weight), (P, c)),
        "ln_b": np.broadcast_to(np.asarray(L1_attn_ln_bias), (P, c)),
        "router_w": np.asarray(L1_ffn_router_w),
        "router_b": np.broadcast_to(np.asarray(L1_ffn_router_b), (P, tiles, experts)),
        "expert_w": expert_weight.transpose(1, 0, 2).reshape(c, -1),
        "expert_b": np.concatenate([np.asarray(L1_ffn_expert_b)] * 3),
        "identity": np.eye(P, dtype=np.float32),
        "group_mean": same_group.astype(np.float32) / np.float32(group),
        "expert_ids": np.broadcast_to(np.arange(experts, dtype=np.float32), (P, tiles, experts)),
        "bias_rows": bias_rows,
    }
    arrays = {k: np.ascontiguousarray(a) for k, a in arrays.items()}
    nc = bacc.Bacc("TRN2", target_bir_lowering=False, num_devices=1)
    aps = {k: nc.dram_tensor(k, a.shape, F32, kind="ExternalInput").ap() for k, a in arrays.items()}
    out = nc.dram_tensor("out", (nb, c, h * w), F32, kind="ExternalOutput").ap()
    build(nc, out=out, **aps)
    result = run_bass_kernel_spmd(nc, [arrays], core_ids=[0])
    return result.results[0]["out"].reshape(nb, c, h, w)
```

```python
from contextlib import ExitStack

import concourse.bass as bass
from concourse import mybir

F32 = mybir.dt.float32
F32R = mybir.dt.float32r
U32 = mybir.dt.uint32
ALU = mybir.AluOpType
ACT = mybir.ActivationFunctionType

P = 128
KS = 3
HALF = 512
GN_EPS, LNT_EPS, ATTN_EPS = 1e-5, 1e-5, 1e-6
SCALE, INV_TEMP = 0.1, 2.0
FIRST, STAGES_AHEAD, STAGES_BEHIND = -2, 3, 4


class Image:

    def __init__(self, pair, c):
        self.n = 2 * pair + c
        self.nth = pair + c // 2
        self.par = c % 2


class Iteration:

    def __init__(self, pair, c, images):
        self.pair, self.c, self.images = pair, c, images
        self.static = isinstance(pair, int)

    def image(self, d):
        if self.static and not 0 <= 2 * self.pair + self.c + d < self.images:
            return None
        return Image(self.pair, self.c + d)


def iterations(eng, images, run):
    last = images + STAGES_BEHIND
    begin = STAGES_BEHIND + 1
    pairs = (images - STAGES_AHEAD - begin) // 2
    for i in range(FIRST, begin):
        run(Iteration(0, i, images))
    with eng.Fori(0, pairs) as pair:
        run(Iteration(pair, begin, images))
        run(Iteration(pair, begin + 1, images))
    for i in range(begin + 2 * pairs, last):
        run(Iteration(0, i, images))


def build(nc, x, conv_w, conv_b, ln_w, ln_b, router_w, router_b, expert_w, expert_b,
          identity, group_mean, expert_ids, bias_rows, out):
    NB, C, HW = x.shape
    W = 32
    H = HW // W
    PW = W + 2
    T = HW // P
    NH = HW // HALF
    TPH = T // NH
    RPH = H // NH
    E = router_w.shape[1]
    TAPS = KS * KS
    STEPS = T

    with ExitStack() as ctx:
        def sb(name, shape, dt=F32):
            return ctx.enter_context(nc.sbuf_tensor(name, shape, dt))

        def psum(name, n=HALF):
            return ctx.enter_context(nc.psum_tensor(name, [P, n], F32))

        def sem(name):
            return ctx.enter_context(nc.semaphore(name))

        ident = sb("ident", [P, P])
        gmat = sb("gmat", [P, P])
        ids = sb("ids", [P, T, E])
        rows24 = sb("rows24", [3 * E, 2])
        cb = sb("cb", [P, 1])
        lnw = sb("lnw", [P, C])
        lnb = sb("lnb", [P, C])
        rb = sb("rb", [P, T, E])
        eb = sb("eb", [3 * E, C])
        ebt = sb("ebt", [3 * E, C])
        eblo = sb("eblo", [3 * E, C])
        ebhi = sb("ebhi", [3 * E, C], F32R)
        ebs = sb("ebs", [3 * E, C], F32R)
        rw = sb("rw", [P, E])
        rwhl = sb("rwhl", [P, 2 * E], F32R)
        rwhi, rwlo = rwhl[:, 0:E], rwhl[:, E:2 * E]
        cwhi = sb("cwhi", [P, TAPS, C], F32R)
        cwlo = sb("cwlo", [P, TAPS, C], F32R)
        ewhi = sb("ewhi", [P, E * C], F32R)
        ewlo = sb("ewlo", [P, E * C], F32R)
        nhalf = sb("nhalf", [P, 1])
        xc = [sb(f"xc_{p}", [P, HW]) for p in range(2)]
        gst = sb("gst", [P, NH, 6])
        gmv = sb("gmv", [P, 2])
        gmean = sb("gmean", [P, 1])
        gdev = sb("gdev", [P, 1])
        gv = sb("gv", [P, 1])
        gve = sb("gve", [P, 1])
        grs = sb("grs", [P, 1])
        gnhi = sb("gnhi", [P, H + 2, PW], F32R)
        gnlo = sb("gnlo", [P, H + 2, PW], F32R)
        x1c = sb("x1c", [P, HW])
        x1t = [sb(f"x1t_{p}", [P, T, C]) for p in range(2)]
        l1st = sb("l1st", [P, T, 6])
        l1mv = [sb(f"l1mv_{p}", [P, T, 2]) for p in range(2)]
        l1ve = sb("l1ve", [P, T])
        l1rs = [sb(f"l1rs_{p}", [P, T]) for p in range(2)]
        l1rec = sb("l1rec", [P, T])
        l1q = sb("l1q", [P, T])
        l1nm = sb("l1nm", [P, T])
        l1n = sb("l1n", [P, T])
        l1in = sb("l1in", [P, T])
        l1a = sb("l1a", [P, T])
        l1nbn = sb("l1nbn", [P, T])
        l1nbu = [sb(f"l1nbu_{p}", [P, T]) for p in range(2)]
        xnhi = [sb(f"xnhi_{p}", [P, HW], F32R) for p in range(2)]
        xnlo = [sb(f"xnlo_{p}", [P, HW], F32R) for p in range(2)]
        es = sb("es", [P, T, HW])
        rsum = [sb(f"rsum_{p}", [P, T]) for p in range(2)]
        rinv = sb("rinv", [P, T])
        rbc = sb("rbc", [P, HW])
        s1 = [sb(f"s1_{p}", [P, HW]) for p in range(2)]
        s1hi = [sb(f"s1hi_{p}", [P, HW], F32R) for p in range(2)]
        s1lo = [sb(f"s1lo_{p}", [P, HW], F32R) for p in range(2)]
        fx = [sb(f"fx_{p}", [P, HW]) for p in range(2)]
        hx = [sb(f"hx_{p}", [P, HW], F32R) for p in range(2)]
        csum = [sb(f"csum_{p}", [P, T]) for p in range(2)]
        ci = [sb(f"ci_{p}", [P, T]) for p in range(2)]
        ci1 = sb("ci1", [P, T])
        u = [sb(f"u_{p}", [P, T, C]) for p in range(2)]
        wf = sb("wf", [P, C])
        whi = [sb(f"whi_{p}", [P, C], F32R) for p in range(2)]
        wlo = [sb(f"wlo_{p}", [P, C], F32R) for p in range(2)]
        yhi = [sb(f"yhi_{p}", [P, C], F32R) for p in range(2)]
        x1b = [sb(f"x1b_{p}", [P, T, C]) for p in range(2)]
        ysum = sb("ysum", [P, 1])
        xneg = sb("xneg", [P, HW])
        yv = sb("yv", [P, T, C])
        outc = yv[:].rearrange("p t c -> p (t c)")
        xnt = yv
        l2st = sb("l2st", [P, T, 6])
        l2mv = sb("l2mv", [P, T, 2])
        l2ve = sb("l2ve", [P, T])
        l2rs = sb("l2rs", [P, T])
        t1 = [sb(f"t1_{p}", [P, T, C]) for p in range(2)]
        l3st = sb("l3st", [P, T, 6])
        l3mv = sb("l3mv", [P, T, 2])
        l3ve = sb("l3ve", [P, T])
        l3rs = sb("l3rs", [P, T])
        l3nm = sb("l3nm", [P, T])
        l3nb = sb("l3nb", [P, T])
        zt = sb("zt", [P, T, C])
        gnf = zt[:].rearrange("p t c -> p (t c)")
        zhi = sb("zhi", [P, HW], F32R)
        zlo = sb("zlo", [P, HW], F32R)
        lgp = sb("lgp", [P, T, E])
        lg = sb("lg", [P, T, E])
        mx = sb("mx", [P, T, 8])
        mi = sb("mi", [P, T, 8], U32)
        mf = sb("mf", [P, 2, T])
        gd = sb("gd", [P, T])
        ge = sb("ge", [P, T])
        gs = sb("gs", [P, T])
        g1 = sb("g1", [P, T])
        g2 = sb("g2", [P, T])
        gm1 = sb("gm1", [P, T, E])
        gm2 = sb("gm2", [P, T, E])
        gate = sb("gate", [P, T, E])
        g24 = sb("g24", [P, T, 3 * E], F32R)
        g24t = sb("g24t", [3 * E, HW], F32R)
        prod = [sb(f"prod_{p}", [P, E * C]) for p in range(2)]

        ps_conv = psum("ps_conv")
        ps_sim = psum("ps_sim", HW)
        ps_att = psum("ps_att", HW)
        ps_ffn = psum("ps_ffn", E * C)
        ps_misc = psum("ps_misc")

        s_const = sem("s_const")
        s_wsplit = sem("s_wsplit")
        s_gnpad = sem("s_gnpad")
        s_nhalf = sem("s_nhalf")
        s_gstats = sem("s_gstats")
        s_gmv = sem("s_gmv")
        s_gmean_ps = sem("s_gmean_ps")
        s_gmeanv = sem("s_gmeanv")
        s_gvar_ps = sem("s_gvar_ps")
        s_gve = sem("s_gve")
        s_grs = sem("s_grs")
        s_gnf = sem("s_gnf")
        s_gnhi = sem("s_gnhi")
        s_gnlo = sem("s_gnlo")
        s_conv_ps = sem("s_conv_ps")
        s_x1c = sem("s_x1c")
        s_x1t_ps = sem("s_x1t_ps")
        s_x1t = sem("s_x1t")
        s_l1st = sem("s_l1st")
        s_l1mv = sem("s_l1mv")
        s_l1ve = sem("s_l1ve")
        s_l1rs = sem("s_l1rs")
        s_l1q = sem("s_l1q")
        s_l1n = sem("s_l1n")
        s_l1a = sem("s_l1a")
        s_xnt = sem("s_xnt")
        s_xn_ps = sem("s_xn_ps")
        s_xnhi = sem("s_xnhi")
        s_xnlo = sem("s_xnlo")
        s_sim_ps = sem("s_sim_ps")
        s_e_tile = sem("s_e_tile")
        s_rinv = sem("s_rinv")
        s_rb_ps = sem("s_rb_ps")
        s_rb = sem("s_rb")
        s_s_tile = sem("s_s_tile")
        s_f_tile = sem("s_f_tile")
        s_s_hi = sem("s_s_hi")
        s_s_lo = sem("s_s_lo")
        s_ci = sem("s_ci")
        s_key_step = sem("s_key_step")
        s_wlo = sem("s_wlo")
        s_h_tile = sem("s_h_tile")
        s_att_ps = sem("s_att_ps")
        s_u_tokens = sem("s_u_tokens")
        s_x1b = sem("s_x1b")
        s_ysum_ps = sem("s_ysum_ps")
        s_ysum = sem("s_ysum")
        s_xneg = sem("s_xneg")
        s_xnegt_ps = sem("s_xnegt_ps")
        s_yv = sem("s_yv")
        s_l2st = sem("s_l2st")
        s_l2mv = sem("s_l2mv")
        s_l2ve = sem("s_l2ve")
        s_l2rs = sem("s_l2rs")
        s_l2q = sem("s_l2q")
        s_t1 = sem("s_t1")
        s_l3st = sem("s_l3st")
        s_l3mv = sem("s_l3mv")
        s_l3ve = sem("s_l3ve")
        s_l3rs = sem("s_l3rs")
        s_l3nb = sem("s_l3nb")
        s_z_tokens = sem("s_z_tokens")
        s_z_ps = sem("s_z_ps")
        s_zhi = sem("s_zhi")
        s_zlo = sem("s_zlo")
        s_logit_ps = sem("s_logit_ps")
        s_lg = sem("s_lg")
        s_mx = sem("s_mx")
        s_mi = sem("s_mi")
        s_gd = sem("s_gd")
        s_ge = sem("s_ge")
        s_gate = sem("s_gate")
        s_gate24 = sem("s_gate24")
        s_gt_ps = sem("s_gt_ps")
        s_gt = sem("s_gt")
        s_gb_ps = sem("s_gb_ps")
        s_t1b = sem("s_t1b")
        s_ffn_ps = sem("s_ffn_ps")
        s_prod = sem("s_prod")
        s_tree = sem("s_tree")
        s_t2 = sem("s_t2")
        s_out_ps = sem("s_out_ps")
        s_outc = sem("s_outc")
        s_stored = sem("s_stored")
        s_loaded = [sem(f"s_loaded{p}") for p in range(2)]

        block = ctx.enter_context(nc.Block())

        def half(ap, h):
            return ap[:, h * HALF:(h + 1) * HALF]

        def tile(ap, t):
            return ap[:, t * P:(t + 1) * P]

        def half_t(ap, h):
            return ap[:, h * TPH:(h + 1) * TPH, :]

        def padded(ap, h, dy=1, dx=1):
            return ap[:, h * RPH + dy:h * RPH + dy + RPH, dx:dx + W]

        def rows(ap):
            return ap.rearrange("p (r w) -> p r w", w=W)

        CONST_LOADS = 12
        WSPLIT = 10
        GMEAN, GATE, FIRST_SCALES, L3, LOGITS = 3, 10, 3, 2, 2
        KEYS, TREE = 2, 3

        def count(value):
            return max(value, 0) if isinstance(value, int) else value

        def dram(ap, it, image):
            return ap[image.n] if it.static else ap[bass.ds(image.n, 1)].rearrange("a p n -> (a p) n")

        @block.sync
        def _(sp):
            es_flat = es[:].rearrange("p t n -> p (t n)")
            loads = [(ident[:], identity), (gmat[:], group_mean), (ids[:], expert_ids), (rows24[:], bias_rows),
                     (cb[:], conv_b), (lnw[:], ln_w), (lnb[:], ln_b), (rb[:], router_b), (eb[:], expert_b),
                     (rw[:], router_w), (es_flat[:, 0:TAPS * C], conv_w),
                     (es_flat[:, TAPS * C:TAPS * C + E * C], expert_w)]
            sp.dma_start(xc[0][:], x[0]).then_inc(s_loaded[0], 16)
            for dst, src in loads:
                sp.dma_start(dst, src).then_inc(s_const, 16)

            def run(it):
                q, ahead = it.image(-4), it.image(3)
                if q:
                    sp.wait_ge(s_outc, NH * q.n + NH)
                    sp.dma_start(dram(out, it, q), outc).then_inc(s_stored, 16)
                if ahead:
                    sp.wait_ge(s_x1c, count(NH * (ahead.n - 2) + NH))
                    sp.dma_start(xc[ahead.par][:], dram(x, it, ahead)).then_inc(s_loaded[ahead.par], 16)

            iterations(sp, NB, run)
            sp.wait_ge(s_stored, 16 * NB)

        @block.tensor
        def _(pe):
            pe.wait_ge(s_const, 16 * CONST_LOADS)
            pe.wait_ge(s_wsplit, WSPLIT)
            mm = nc.tensor.matmul
            PARTS = 3

            def run(it):
                a, b, c, v, w, o, q = (it.image(d) for d in (2, 1, 0, -1, -2, -3, -4))

                if c:
                    reader = (s_xnlo, NH * c.n + NH)
                elif o:
                    reader = (s_yv, NH * o.n + NH)
                elif q:
                    reader = (s_t1b, NH * q.n + NH)
                elif b:
                    reader = (s_gve, b.n + 1)
                else:
                    reader = (s_gve, 0)

                def sim(t):
                    pe.wait_ge(s_xnlo, NH * c.n + NH)
                    pe.wait_ge(s_e_tile, T * c.n + t)
                    hi, lo = xnhi[c.par], xnlo[c.par]
                    for h in range(NH):
                        mm(half(ps_sim, h), tile(hi, t), half(hi, h), start=True, stop=False)
                        mm(half(ps_sim, h), tile(hi, t), half(lo, h), start=False, stop=False)
                        m = mm(half(ps_sim, h), tile(lo, t), half(hi, h), start=False, stop=True)
                    m.then_inc(s_sim_ps, 1)

                def conv(g, h, first, last):
                    for n in range(first, last):
                        tap, part = divmod(n, PARTS)
                        if n == 0:
                            pe.wait_ge(s_gnhi, g.n + 1)
                            pe.wait_ge(s_gnlo, g.n + 1)
                            pe.wait_ge(s_x1c, NH * g.n + h)
                        wts, src = ((cwhi, gnhi), (cwhi, gnlo), (cwlo, gnhi))[part]
                        m = mm(rows(ps_conv[:]), wts[:, tap, :], padded(src, h, tap // KS, tap % KS),
                               start=(n == 0), stop=(n == TAPS * PARTS - 1))
                        if n == TAPS * PARTS - 1:
                            m.then_inc(s_conv_ps, 1)

                def attend(g, k):
                    pe.wait_ge(s_s_hi, T * g.n + k + 1)
                    pe.wait_ge(s_s_lo, T * g.n + k + 1)
                    pe.wait_ge(s_wlo, T * g.n + k + 1)
                    pe.wait_ge(s_h_tile, T * g.n + k + 1)
                    if k == 0:
                        pe.wait_ge(s_xneg, NH * g.n)
                    r = k % 2
                    for h in range(NH):
                        mm(half(ps_att, h), whi[r][:], half(s1hi[r], h), start=(k == 0), stop=False)
                        mm(half(ps_att, h), whi[r][:], half(s1lo[r], h), start=False, stop=False)
                        mm(half(ps_att, h), wlo[r][:], half(s1hi[r], h), start=False, stop=False)
                        m = mm(half(ps_att, h), yhi[r][:], half(hx[r], h), start=False, stop=(k == T - 1))
                    m.then_inc(s_att_ps, 1)

                def ffn(t):
                    pe.wait_ge(s_zlo, NH * o.n + NH)
                    pe.wait_ge(s_prod, T * o.n + t)
                    for h in range(NH):
                        mm(half(ps_ffn, h), tile(zhi, t), half(ewhi, h), start=True, stop=False)
                        mm(half(ps_ffn, h), tile(zhi, t), half(ewlo, h), start=False, stop=False)
                        m = mm(half(ps_ffn, h), tile(zlo, t), half(ewhi, h), start=False, stop=True)
                    m.then_inc(s_ffn_ps, 1)

                def transposes(src_tile, h):
                    for j in range(TPH):
                        m = nc.tensor.transpose(tile(ps_misc, j), src_tile(h * TPH + j), ident[:])
                    return m

                def misc_rb(h):
                    nonlocal reader
                    pe.wait_ge(s_rinv, v.n + 1)
                    pe.wait_ge(*reader)
                    reader = (s_rb, NH * v.n + h + 1)
                    transposes(lambda t: rinv[:, t:t + 1].to_broadcast([P, P]), h).then_inc(s_rb_ps, 1)

                def misc_ysum():
                    nonlocal reader
                    pe.wait_ge(s_ci, T * w.n + T)
                    pe.wait_ge(*reader)
                    reader = (s_ysum, w.n + 1)
                    for t in range(T):
                        m = mm(ps_misc[:, 0:1], u[w.par][:, t, :], ci[w.par][:, t:t + 1],
                               start=(t == 0), stop=(t == T - 1))
                    m.then_inc(s_ysum_ps, 1)

                def misc_out(h):
                    nonlocal reader
                    pe.wait_ge(s_t2, T * q.n + (h + 1) * TPH)
                    pe.wait_ge(*reader)
                    reader = (s_outc, NH * q.n + h + 1)
                    transposes(lambda t: t1[q.par][:, t, :], h).then_inc(s_out_ps, 1)

                def misc_xneg(h):
                    nonlocal reader
                    pe.wait_ge(s_xneg, NH * w.n + h + 1)
                    pe.wait_ge(*reader)
                    reader = (s_yv, NH * w.n + h + 1)
                    transposes(lambda t: tile(xneg, t), h).then_inc(s_xnegt_ps, 1)

                def misc_z(h):
                    nonlocal reader
                    pe.wait_ge(s_z_tokens, NH * o.n + h + 1)
                    pe.wait_ge(*reader)
                    reader = (s_zlo, NH * o.n + h + 1)
                    transposes(lambda t: zt[:, t, :], h).then_inc(s_z_ps, 1)

                def misc_router():
                    nonlocal reader
                    pe.wait_ge(s_zlo, NH * o.n + NH)
                    pe.wait_ge(*reader)
                    reader = (s_lg, LOGITS * o.n + LOGITS)
                    for t in range(T):
                        at = 2 * E * t
                        mm(ps_misc[:, at:at + 2 * E], tile(zhi, t), rwhl[:], start=True, stop=False)
                        m = mm(ps_misc[:, at:at + E], tile(zlo, t), rwhi, start=False, stop=True)
                    m.then_inc(s_logit_ps, 1)

                def misc_gmean():
                    nonlocal reader
                    pe.wait_ge(s_gmv, a.n + 1)
                    pe.wait_ge(*reader)
                    reader = (s_gmeanv, GMEAN * a.n + 1)
                    mm(ps_misc[:, 0:1], gmat[:], gmv[:, 0:1], start=True, stop=True).then_inc(s_gmean_ps, 1)

                def misc_gvar():
                    nonlocal reader
                    pe.wait_ge(s_gmeanv, GMEAN * a.n + GMEAN)
                    pe.wait_ge(*reader)
                    reader = (s_gve, a.n + 1)
                    mm(ps_misc[:, 0:1], gmat[:], gv[:], start=True, stop=True).then_inc(s_gvar_ps, 1)

                def misc_x1(h):
                    nonlocal reader
                    pe.wait_ge(s_x1c, NH * b.n + h + 1)
                    pe.wait_ge(*reader)
                    reader = (s_x1t, NH * b.n + h + 1)
                    transposes(lambda t: tile(x1c, t), h).then_inc(s_x1t_ps, 1)

                def misc_gt(h):
                    nonlocal reader
                    pe.wait_ge(s_gate24, o.n + 1)
                    pe.wait_ge(*reader)
                    reader = (s_gt, NH * o.n + h + 1)
                    for j in range(TPH):
                        m = nc.tensor.transpose(tile(ps_misc, j)[0:3 * E, :],
                                                g24[:, h * TPH + j, :].bitcast(F32), ident[:])
                    m.then_inc(s_gt_ps, 1)

                def misc_gb(h):
                    nonlocal reader
                    pe.wait_ge(s_gt, NH * o.n + h + 1)
                    pe.wait_ge(*reader)
                    reader = (s_t1b, NH * o.n + h + 1)
                    for j in range(TPH):
                        m = mm(tile(ps_misc, j), tile(g24t, h * TPH + j), ebs[:], start=True, stop=True)
                    m.then_inc(s_gb_ps, 1)

                def misc_xn(h):
                    nonlocal reader
                    pe.wait_ge(s_xnt, NH * b.n + h + 1)
                    pe.wait_ge(*reader)
                    reader = (s_xnlo, NH * b.n + h + 1)
                    transposes(lambda t: xnt[:, t, :], h).then_inc(s_xn_ps, 1)

                if c:
                    sim(0)
                if v:
                    misc_rb(0)
                    misc_rb(1)
                if b:
                    conv(b, 1, 0, 9)
                if o:
                    misc_z(0)
                if w:
                    attend(w, T - 2)
                if o:
                    misc_z(1)
                    misc_router()
                if c:
                    sim(1)
                if a:
                    misc_gmean()
                if b:
                    conv(b, 1, 9, 18)
                if o:
                    ffn(0)
                if w:
                    attend(w, T - 1)
                    misc_ysum()
                if q:
                    misc_out(0)
                if c:
                    sim(2)
                if q:
                    misc_out(1)
                if a:
                    misc_gvar()
                if b:
                    conv(b, 1, 18, 27)
                if o:
                    misc_gt(0)
                    ffn(1)
                if b:
                    misc_x1(0)
                if o:
                    misc_gt(1)
                if v:
                    attend(v, 0)
                if c:
                    sim(3)
                if w:
                    misc_xneg(0)
                if o:
                    misc_gb(0)
                    ffn(2)
                    misc_gb(1)
                if v:
                    attend(v, 1)
                if b:
                    misc_x1(1)
                if c:
                    sim(4)
                if w:
                    misc_xneg(1)
                if o:
                    ffn(3)
                if v:
                    attend(v, 2)
                if c:
                    sim(5)
                if a:
                    conv(a, 0, 0, 9)
                if o:
                    ffn(4)
                if v:
                    attend(v, 3)
                if c:
                    sim(6)
                if a:
                    conv(a, 0, 9, 18)
                if o:
                    ffn(5)
                if v:
                    attend(v, 4)
                if c:
                    sim(7)
                if a:
                    conv(a, 0, 18, 23)
                if b:
                    misc_xn(0)
                if o:
                    ffn(6)
                if a:
                    conv(a, 0, 23, 27)
                if b:
                    misc_xn(1)
                if v:
                    attend(v, 5)
                if o:
                    ffn(7)

            iterations(pe, NB, run)

        @block.scalar
        def _(act):
            act.wait_ge(s_gnpad, 2)
            act.wait_ge(s_wsplit, WSPLIT)

            def run(it):
                a, b, c, v, w, o, q = (it.image(d) for d in (2, 1, 0, -1, -2, -3, -4))

                def exp_sim(t):
                    act.wait_ge(s_sim_ps, T * c.n + t + 1)
                    if v:
                        act.wait_ge(s_s_tile, T * v.n + t + 1)
                    nc.scalar.activation(es[:, t, :], ps_sim[:], ACT.Exp, scale=INV_TEMP,
                                         accum_out=rsum[c.par][:, t:t + 1]).then_inc(s_e_tile, 1)

                def exp_s(g, t):
                    act.wait_ge(s_s_tile, T * g.n + t + 1)
                    act.wait_ge(s_h_tile, count(T * g.n + t - 1))
                    nc.scalar.activation(fx[t % 2][:], s1[t % 2][:], ACT.Exp,
                                         accum_out=csum[g.par][:, t:t + 1]).then_inc(s_f_tile, 1)

                def round_s(g, t):
                    act.wait_ge(s_att_ps, count(T * g.n + t - 1))
                    nc.scalar.copy(s1hi[t % 2][:], s1[t % 2][:]).then_inc(s_s_hi, 1)

                def rb_copy(h):
                    act.wait_ge(s_rb_ps, NH * v.n + h + 1)
                    act.wait_ge(s_s_tile, T * v.n)
                    nc.scalar.copy(half(rbc, h), ps_misc[:]).then_inc(s_rb, 1)

                def ysum_copy():
                    act.wait_ge(s_ysum_ps, w.n + 1)
                    act.wait_ge(s_xneg, NH * w.n)
                    nc.scalar.copy(ysum[:], ps_misc[:, 0:1]).then_inc(s_ysum, 1)

                def xneg_copy(h):
                    act.wait_ge(s_ysum, w.n + 1)
                    act.wait_ge(s_att_ps, T * w.n + T)
                    act.wait_ge(s_xnegt_ps, NH * w.n)
                    nc.scalar.activation(half(xneg, h), half(ps_att, h), ACT.Identity,
                                         bias=ysum[:]).then_inc(s_xneg, 1)

                def out_copy(h):
                    act.wait_ge(s_out_ps, NH * q.n + h + 1)
                    act.wait_ge(s_stored, 16 * q.n)
                    if c:
                        act.wait_ge(s_xn_ps, NH * c.n + NH)
                    nc.scalar.copy(outc[:, h * HALF:(h + 1) * HALF], ps_misc[:]).then_inc(s_outc, 1)

                def x1_copy(h):
                    act.wait_ge(s_x1t_ps, NH * b.n + h + 1)
                    act.wait_ge(s_x1b, count(b.n - 1))
                    act.wait_ge(s_u_tokens, count(b.n - 1))
                    nc.scalar.copy(half(x1t[b.par][:].rearrange("p t c -> p (t c)"), h), ps_misc[:]).then_inc(s_x1t, 1)

                def z_round(h):
                    act.wait_ge(s_z_ps, NH * o.n + h + 1)
                    act.wait_ge(s_ffn_ps, T * o.n)
                    nc.scalar.copy(half(zhi, h), ps_misc[:]).then_inc(s_zhi, 1)

                def gate_copy(h):
                    act.wait_ge(s_gt_ps, NH * o.n + h + 1)
                    act.wait_ge(s_gb_ps, NH * o.n)
                    nc.scalar.copy(half(g24t, h), ps_misc[0:3 * E, :]).then_inc(s_gt, 1)

                def xn_round(h):
                    act.wait_ge(s_xn_ps, NH * b.n + h + 1)
                    act.wait_ge(s_sim_ps, count(T * (b.n - 1)))
                    nc.scalar.copy(half(xnhi[b.par], h), ps_misc[:]).then_inc(s_xnhi, 1)

                def unit_tokens():
                    act.wait_ge(s_x1t, NH * v.n + NH)
                    act.wait_ge(s_l1a, FIRST_SCALES * v.n + FIRST_SCALES)
                    act.wait_ge(s_yv, count(NH * (v.n - 2) + NH))
                    act.wait_ge(s_ysum_ps, count(v.n - 1))
                    for t in range(T):
                        i_ = nc.scalar.activation(u[v.par][:, t, :], x1t[v.par][:, t, :], ACT.Identity,
                                                  scale=l1rs[v.par][:, t:t + 1], bias=l1nbu[v.par][:, t:t + 1])
                    i_.then_inc(s_u_tokens, 1)

                def normalise(h):
                    act.wait_ge(s_l1a, FIRST_SCALES * b.n + FIRST_SCALES)
                    act.wait_ge(s_x1t, NH * b.n + NH)
                    act.wait_ge(s_xn_ps, NH * b.n)
                    if w:
                        act.wait_ge(s_t1, NH * w.n + h + 1)
                    for t in range(h * TPH, (h + 1) * TPH):
                        i_ = nc.scalar.activation(xnt[:, t, :], x1t[b.par][:, t, :], ACT.Identity,
                                                  scale=l1a[:, t:t + 1], bias=l1nbn[:, t:t + 1])
                    i_.then_inc(s_xnt, 1)

                def z_tokens(g, h):
                    act.wait_ge(s_l3nb, g.n + 1)
                    act.wait_ge(s_z_ps, NH * g.n)
                    if a and h == 0:
                        act.wait_ge(s_gnlo, a.n + 1)
                    for t in range(h * TPH, (h + 1) * TPH):
                        i_ = nc.scalar.activation(zt[:, t, :], t1[g.par][:, t, :], ACT.Identity,
                                                  scale=l3rs[:, t:t + 1], bias=l3nb[:, t:t + 1])
                    i_.then_inc(s_z_tokens, 1)

                if v:
                    rb_copy(0)
                    rb_copy(1)
                if o:
                    z_tokens(o, 1)
                if w:
                    round_s(w, T - 1)
                if o:
                    z_round(0)
                if c:
                    exp_sim(0)
                if v:
                    exp_s(v, 0)
                if o:
                    z_round(1)
                if v:
                    round_s(v, 0)
                if c:
                    exp_sim(1)
                if v:
                    exp_s(v, 1)
                    unit_tokens()
                if o:
                    act.wait_ge(s_gd, o.n + 1)
                    nc.scalar.activation(ge[:], gd[:], ACT.Exp).then_inc(s_ge, 1)
                if w:
                    ysum_copy()
                if q:
                    out_copy(0)
                if w:
                    xneg_copy(0)
                    xneg_copy(1)
                if v:
                    round_s(v, 1)
                if q:
                    out_copy(1)
                if c:
                    exp_sim(2)
                if v:
                    exp_s(v, 2)
                if o:
                    gate_copy(0)
                if b:
                    x1_copy(0)
                if o:
                    gate_copy(1)
                if v:
                    round_s(v, 2)
                if c:
                    exp_sim(3)
                if v:
                    exp_s(v, 3)
                if a:
                    act.wait_ge(s_gnf, a.n + 1)
                    if b:
                        act.wait_ge(s_conv_ps, NH * b.n + NH)
                    nc.scalar.copy(gnhi[:, 1:1 + H, 1:1 + W], rows(gnf)).then_inc(s_gnhi, 1)
                if b:
                    x1_copy(1)
                if v:
                    round_s(v, 3)
                if c:
                    exp_sim(4)
                if v:
                    exp_s(v, 4)
                if v:
                    round_s(v, 4)
                if c:
                    exp_sim(5)
                if v:
                    exp_s(v, 5)
                if v:
                    round_s(v, 5)
                if c:
                    exp_sim(6)
                if v:
                    exp_s(v, 6)
                if b:
                    normalise(0)
                    normalise(1)
                if v:
                    round_s(v, 6)
                if b:
                    xn_round(0)
                if c:
                    exp_sim(7)
                if v:
                    exp_s(v, 7)
                if b:
                    xn_round(1)
                if w:
                    z_tokens(w, 0)

            iterations(act, NB, run)

        @block.gpsimd
        def _(pool):
            add = nc.gpsimd.tensor_tensor
            nc.gpsimd.memset(nhalf[:], -0.5).then_inc(s_nhalf, 1)
            nc.gpsimd.memset(gnhi[:].bitcast(F32), 0.0).then_inc(s_gnpad, 1)
            nc.gpsimd.memset(gnlo[:].bitcast(F32), 0.0).then_inc(s_gnpad, 1)
            pool.wait_ge(s_nhalf, 1)
            pool.wait_ge(s_const, 16 * CONST_LOADS)

            def run(it):
                a, b, c, v, w, o, q = (it.image(d) for d in (2, 1, 0, -1, -2, -3, -4))

                def inv_sqrt(dst, src):
                    return nc.gpsimd.tensor_tensor(dst, src, nhalf[:].to_broadcast([P, src.shape[1]]), ALU.pow)

                def low_s(g, t):
                    pool.wait_ge(s_s_hi, T * g.n + t + 1)
                    pool.wait_ge(s_att_ps, count(T * g.n + t - 1))
                    nc.gpsimd.tensor_tensor(s1lo[t % 2][:], s1[t % 2][:], s1hi[t % 2][:].bitcast(F32),
                                            ALU.subtract).then_inc(s_s_lo, 1)

                def expert_tree(g, t):
                    p = prod[t % 2]
                    pool.wait_ge(s_prod, T * g.n + t + 1)
                    for k in range(TREE):
                        n = E * C >> (k + 1)
                        add(p[:, 0:n], p[:, 0:n], p[:, n:2 * n], ALU.add).then_inc(s_tree, 1)
                        pool.wait_ge(s_tree, TREE * (T * g.n + t) + k + 1)

                def expert_add(g, t):
                    pool.wait_ge(s_t1b, NH * g.n + NH)
                    add(t1[g.par][:, t, :], t1[g.par][:, t, :], prod[t % 2][:, 0:C], ALU.add).then_inc(s_t2, 1)

                def first_scales():
                    pool.wait_ge(s_l1ve, b.n + 1)
                    pool.wait_ge(s_u_tokens, count(b.n - 1))
                    inv_sqrt(l1rs[b.par][:], l1ve[:]).then_inc(s_l1rs, 1)
                    pool.wait_ge(s_l1q, 3 * b.n + 3)
                    inv_sqrt(l1in[:], l1n[:]).then_inc(s_l1n, 1)
                    pool.wait_ge(s_l1rs, b.n + 1)
                    pool.wait_ge(s_l1n, b.n + 1)
                    pool.wait_ge(s_xnt, NH * b.n)
                    mul = nc.gpsimd.tensor_tensor
                    mul(l1a[:], l1rs[b.par][:], l1in[:], ALU.mult).then_inc(s_l1a, 1)
                    mul(l1nbu[b.par][:], l1nm[:], l1rs[b.par][:], ALU.mult).then_inc(s_l1a, 1)
                    pool.wait_ge(s_l1a, FIRST_SCALES * b.n + 1)
                    mul(l1nbn[:], l1nm[:], l1a[:], ALU.mult).then_inc(s_l1a, 1)

                if w:
                    low_s(w, T - 1)
                if q:
                    expert_tree(q, T - 2)
                    expert_add(q, T - 2)
                    expert_tree(q, T - 1)
                    expert_add(q, T - 1)
                if v:
                    low_s(v, 0)
                    pool.wait_ge(s_x1t, NH * v.n + NH)
                    pool.wait_ge(s_t1, count(NH * (v.n - 2) + NH))
                    add(x1b[v.par][:], x1t[v.par][:], lnb[:].unsqueeze(1).to_broadcast([P, T, C]),
                        ALU.add).then_inc(s_x1b, 1)
                if v:
                    low_s(v, 1)
                if a:
                    pool.wait_ge(s_gve, a.n + 1)
                    inv_sqrt(grs[:], gve[:]).then_inc(s_grs, 1)
                if o:
                    expert_tree(o, 0)
                if v:
                    low_s(v, 2)
                if o:
                    expert_add(o, 0)
                    expert_tree(o, 1)
                    expert_add(o, 1)
                if v:
                    low_s(v, 3)
                if o:
                    expert_tree(o, 2)
                    expert_add(o, 2)
                if w:
                    pool.wait_ge(s_l2ve, w.n + 1)
                    inv_sqrt(l2rs[:], l2ve[:]).then_inc(s_l2rs, 1)
                if v:
                    low_s(v, 4)
                if b:
                    first_scales()
                if o:
                    expert_tree(o, 3)
                    expert_add(o, 3)
                if v:
                    low_s(v, 5)
                if o:
                    expert_tree(o, 4)
                    expert_add(o, 4)
                if w:
                    pool.wait_ge(s_l3ve, L3 * w.n + L3)
                    pool.wait_ge(s_z_tokens, NH * w.n)
                    inv_sqrt(l3rs[:], l3ve[:]).then_inc(s_l3rs, 1)
                    pool.wait_ge(s_l3rs, w.n + 1)
                    nc.gpsimd.tensor_tensor(l3nb[:], l3nm[:], l3rs[:], ALU.mult).then_inc(s_l3nb, 1)
                if v:
                    low_s(v, 6)
                if o:
                    expert_tree(o, 5)
                    expert_add(o, 5)

            iterations(pool, NB, run)

        @block.vector
        def _(dve):
            V = nc.vector
            es_flat = es[:].rearrange("p t n -> p (t n)")
            dve.wait_ge(s_const, 16 * CONST_LOADS)
            cw = es_flat[:, 0:TAPS * C]
            ew = es_flat[:, TAPS * C:TAPS * C + E * C]
            cwh, cwl = (ap[:].rearrange("p a b -> p (a b)") for ap in (cwhi, cwlo))
            V.tensor_copy(cwh, cw).then_inc(s_wsplit, 1)
            V.tensor_copy(ewhi[:], ew).then_inc(s_wsplit, 1)
            V.tensor_copy(rwhi, rw[:]).then_inc(s_wsplit, 1)
            V.tensor_copy(ebhi[:], eb[:]).then_inc(s_wsplit, 1)
            dve.wait_ge(s_wsplit, 4)
            V.tensor_tensor(cwl, cw, cwh.bitcast(F32), ALU.subtract).then_inc(s_wsplit, 1)
            V.tensor_tensor(ewlo[:], ew, ewhi[:].bitcast(F32), ALU.subtract).then_inc(s_wsplit, 1)
            V.tensor_tensor(rwlo, rw[:], rwhi.bitcast(F32), ALU.subtract).then_inc(s_wsplit, 1)
            V.tensor_tensor(eblo[:], eb[:], ebhi[:].bitcast(F32), ALU.subtract).then_inc(s_wsplit, 1)
            dve.wait_ge(s_wsplit, 8)
            V.tensor_scalar(ebt[:], eblo[:], rows24[:, 1:2], None, ALU.mult).then_inc(s_wsplit, 1)
            dve.wait_ge(s_wsplit, 9)
            V.scalar_tensor_tensor(out=ebs[:], in0=ebhi[:].bitcast(F32), scalar=rows24[:, 0:1], in1=ebt[:],
                                   op0=ALU.mult, op1=ALU.add).then_inc(s_wsplit, 1)

            def run(it):
                a, b, c, v, w, o, q = (it.image(d) for d in (2, 1, 0, -1, -2, -3, -4))

                def flat(ap, h):
                    return half_t(ap, h).rearrange("p t c -> p (t c)")

                def of_half(h):
                    return range(h * TPH, (h + 1) * TPH)

                def token_stats(src, st, mv, h, g, st_done, mv_done):
                    for t in of_half(h):
                        i_ = V.bn_stats(st[:, t, :], src[:, t, :])
                    i_.then_inc(st_done, 1)
                    dve.wait_ge(s_wsplit, 1)
                    dve.wait_ge(st_done, NH * g.n + h + 1)
                    for t in of_half(h):
                        i_ = V.bn_aggr(mv[:, t, :], st[:, t, :])
                    i_.then_inc(mv_done, 1)

                def scale_rows(k):
                    dve.wait_ge(s_rb, NH * v.n + NH)
                    dve.wait_ge(s_s_lo, count(T * v.n + k - 1))
                    dve.wait_ge(s_f_tile, count(T * v.n + k - 1))
                    dve.wait_ge(s_h_tile, count(T * v.n + k - 1))
                    V.tensor_tensor(s1[k % 2][:], es[:, k, :], rbc[:], ALU.mult).then_inc(s_s_tile, 1)

                def key_rest(g, k):
                    n = T * g.n + k
                    dve.wait_ge(s_f_tile, n + 1)
                    V.reciprocal(ci[g.par][:, k:k + 1], csum[g.par][:, k:k + 1]).then_inc(s_ci, 1)
                    dve.wait_ge(s_att_ps, count(n - 1))
                    V.scalar_tensor_tensor(out=hx[k % 2][:], in0=fx[k % 2][:], scalar=-1.0, in1=s1[k % 2][:],
                                           op0=ALU.add, op1=ALU.subtract).then_inc(s_h_tile, 1)

                def key_tokens(g, k):
                    r = k % 2
                    n = T * g.n + k
                    cik, uk = ci[g.par][:, k:k + 1], u[g.par][:, k, :]
                    dve.wait_ge(s_ci, n + 1)
                    dve.wait_ge(s_att_ps, count(n - 1))
                    dve.wait_ge(s_wlo, n)
                    V.tensor_scalar(ci1[:, k:k + 1], cik, 1.0, None, ALU.add).then_inc(s_key_step, 1)
                    dve.wait_ge(s_u_tokens, g.n + 1)
                    V.tensor_scalar(yhi[r][:], uk, cik, None, ALU.mult)
                    dve.wait_ge(s_key_step, KEYS * n + 1)
                    V.tensor_scalar(wf[:], uk, ci1[:, k:k + 1], None, ALU.mult)
                    V.tensor_scalar(whi[r][:], uk, ci1[:, k:k + 1], None, ALU.mult).then_inc(s_key_step, 1)
                    dve.wait_ge(s_key_step, KEYS * n + 2)
                    V.tensor_tensor(wlo[r][:], wf[:], whi[r][:].bitcast(F32), ALU.subtract).then_inc(s_wlo, 1)

                def attention_residual(h):
                    dve.wait_ge(s_xnegt_ps, NH * w.n + h + 1)
                    if c:
                        dve.wait_ge(s_xn_ps, NH * c.n + NH)
                    if q:
                        dve.wait_ge(s_stored, 16 * q.n + 16)
                    V.scalar_tensor_tensor(out=flat(yv, h), in0=ps_misc[:], scalar=-SCALE,
                                           in1=flat(u[w.par], h), op0=ALU.mult, op1=ALU.add).then_inc(s_yv, 1)

                def attention_stats(h):
                    dve.wait_ge(s_yv, NH * w.n + h + 1)
                    token_stats(yv, l2st, l2mv, h, w, s_l2st, s_l2mv)
                    if h == NH - 1:
                        dve.wait_ge(s_l2mv, NH * w.n + NH)
                        V.tensor_scalar(l2ve[:], l2mv[:, :, 1], ATTN_EPS, None, ALU.add).then_inc(s_l2ve, 1)

                def residual_norm(h):
                    dve.wait_ge(s_l2rs, w.n + 1)
                    dve.wait_ge(s_x1b, w.n + 1)
                    dve.wait_ge(s_out_ps, count(NH * (w.n - 2) + NH))
                    for t in of_half(h):
                        i_ = V.scalar_tensor_tensor(out=yv[:, t, :], in0=yv[:, t, :], scalar=l2mv[:, t, 0:1],
                                                    in1=lnw[:], op0=ALU.subtract, op1=ALU.mult)
                    i_.then_inc(s_l2q, 1)
                    dve.wait_ge(s_l2q, NH * w.n + h + 1)
                    for t in of_half(h):
                        i_ = V.scalar_tensor_tensor(out=t1[w.par][:, t, :], in0=yv[:, t, :], scalar=l2rs[:, t:t + 1],
                                                    in1=x1b[w.par][:, t, :], op0=ALU.mult, op1=ALU.add)
                    i_.then_inc(s_t1, 1)
                    dve.wait_ge(s_t1, NH * w.n + h + 1)
                    token_stats(t1[w.par], l3st, l3mv, h, w, s_l3st, s_l3mv)
                    if h == NH - 1:
                        dve.wait_ge(s_l3mv, NH * w.n + NH)
                        V.tensor_scalar(l3ve[:], l3mv[:, :, 1], LNT_EPS, None, ALU.add).then_inc(s_l3ve, 1)
                        V.tensor_scalar(l3nm[:], l3mv[:, :, 0], -1.0, None, ALU.mult).then_inc(s_l3ve, 1)

                def two_largest():
                    dve.wait_ge(s_wsplit, 1)
                    dve.wait_ge(s_lg, LOGITS * o.n + LOGITS)
                    for t in range(T):
                        i_ = V.max(mx[:, t, :], lg[:, t, :])
                    i_.then_inc(s_mx, 1)
                    dve.wait_ge(s_mx, o.n + 1)
                    V.tensor_tensor(gd[:], mx[:, :, 1], mx[:, :, 0], ALU.subtract).then_inc(s_gd, 1)
                    for t in range(T):
                        i_ = V.max_index(mi[:, t, :], mx[:, t, :], lg[:, t, :])
                    i_.then_inc(s_mi, 1)
                    dve.wait_ge(s_mi, NH * o.n + 1)
                    V.tensor_copy(mf[:].rearrange("p k t -> p t k"), mi[:, :, 0:2]).then_inc(s_mi, 1)

                def gates():
                    def wide(ap):
                        return ap.unsqueeze(2).to_broadcast([P, T, E])

                    g0 = GATE * o.n
                    dve.wait_ge(s_mi, 2 * o.n + 2)
                    V.tensor_tensor(gm1[:], ids[:], wide(mf[:, 0, :]), ALU.is_equal).then_inc(s_gate, 1)
                    V.tensor_tensor(gm2[:], ids[:], wide(mf[:, 1, :]), ALU.is_equal).then_inc(s_gate, 1)
                    dve.wait_ge(s_ge, o.n + 1)
                    V.tensor_scalar(gs[:], ge[:], 1.0, None, ALU.add).then_inc(s_gate, 1)
                    dve.wait_ge(s_gate, g0 + 3)
                    V.reciprocal(g1[:], gs[:]).then_inc(s_gate, 1)
                    dve.wait_ge(s_gate, g0 + 4)
                    V.tensor_tensor(g2[:], ge[:], g1[:], ALU.mult).then_inc(s_gate, 1)
                    V.tensor_tensor(gm1[:], gm1[:], wide(g1[:]), ALU.mult).then_inc(s_gate, 1)
                    dve.wait_ge(s_gate, g0 + 6)
                    V.tensor_tensor(gm2[:], gm2[:], wide(g2[:]), ALU.mult).then_inc(s_gate, 1)
                    dve.wait_ge(s_gate, g0 + 7)
                    V.tensor_tensor(gate[:], gm1[:], gm2[:], ALU.add).then_inc(s_gate, 1)
                    dve.wait_ge(s_gate, g0 + 8)
                    dve.wait_ge(s_gt_ps, NH * o.n)
                    V.tensor_copy(g24[:, :, 0:E], gate[:]).then_inc(s_gate, 1)
                    V.tensor_copy(g24[:, :, 2 * E:3 * E], gate[:]).then_inc(s_gate, 1)
                    dve.wait_ge(s_gate, g0 + 9)
                    V.tensor_tensor(g24[:, :, E:2 * E], gate[:], g24[:, :, 0:E].bitcast(F32),
                                    ALU.subtract).then_inc(s_gate24, 1)

                def gated_bias(h):
                    dve.wait_ge(s_gb_ps, NH * o.n + h + 1)
                    V.tensor_tensor(flat(t1[o.par], h), flat(t1[o.par], h), ps_misc[:], ALU.add).then_inc(s_t1b, 1)

                def gate_experts(g, t):
                    dve.wait_ge(s_gate, GATE * g.n + 8)
                    dve.wait_ge(s_ffn_ps, T * g.n + t + 1)
                    dve.wait_ge(s_t2, count(T * g.n + t - 1))
                    V.tensor_tensor(prod[t % 2][:].rearrange("p (e c) -> p e c", e=E),
                                    ps_ffn[:].rearrange("p (e c) -> p e c", e=E),
                                    gate[:, t, :].unsqueeze(2).to_broadcast([P, E, C]),
                                    ALU.mult).then_inc(s_prod, 1)

                def conv_out(h):
                    dve.wait_ge(s_conv_ps, NH * b.n + h + 1)
                    dve.wait_ge(s_x1t_ps, NH * b.n)
                    dve.wait_ge(s_loaded[b.par], 16 * b.nth + 16)
                    V.scalar_tensor_tensor(out=half(x1c, h), in0=ps_conv[:], scalar=cb[:], in1=half(xc[b.par], h),
                                           op0=ALU.add, op1=ALU.add).then_inc(s_x1c, 1)

                def first_stats(h):
                    dve.wait_ge(s_x1t, NH * b.n + h + 1)
                    token_stats(x1t[b.par], l1st, l1mv[b.par], h, b, s_l1st, s_l1mv)

                def first_norms():
                    dve.wait_ge(s_l1mv, NH * b.n + NH)
                    V.tensor_scalar(l1ve[:], l1mv[b.par][:, :, 1], LNT_EPS, None, ALU.add).then_inc(s_l1ve, 1)
                    dve.wait_ge(s_l1ve, b.n + 1)
                    V.reciprocal(l1rec[:], l1ve[:]).then_inc(s_l1q, 1)
                    dve.wait_ge(s_l1q, 3 * b.n + 1)
                    V.scalar_tensor_tensor(out=l1q[:], in0=l1rec[:], scalar=float(C), in1=l1mv[b.par][:, :, 1],
                                           op0=ALU.mult, op1=ALU.mult).then_inc(s_l1q, 1)
                    dve.wait_ge(s_l1q, 3 * b.n + 2)
                    V.tensor_scalar(l1nm[:], l1mv[b.par][:, :, 0], -1.0, None, ALU.mult)
                    V.tensor_scalar(l1n[:], l1q[:], 1e-24, None, ALU.max).then_inc(s_l1q, 1)

                def low_xn(h):
                    dve.wait_ge(s_xnhi, NH * b.n + h + 1)
                    V.tensor_tensor(half(xnlo[b.par], h), ps_misc[:], half(xnhi[b.par], h).bitcast(F32),
                                    ALU.subtract).then_inc(s_xnlo, 1)

                def low_z(h):
                    dve.wait_ge(s_zhi, NH * o.n + h + 1)
                    V.tensor_tensor(half(zlo, h), ps_misc[:], half(zhi, h).bitcast(F32),
                                    ALU.subtract).then_inc(s_zlo, 1)

                if v:
                    dve.wait_ge(s_e_tile, T * v.n + T)
                    dve.wait_ge(s_rb_ps, NH * v.n)
                    V.reciprocal(rinv[:], rsum[v.par][:]).then_inc(s_rinv, 1)
                if b:
                    conv_out(0)
                if w:
                    key_rest(w, T - 2)
                    key_tokens(w, T - 2)
                if q:
                    gate_experts(q, T - 1)
                if v:
                    scale_rows(0)
                if a:
                    dve.wait_ge(s_loaded[a.par], 16 * a.nth + 16)
                    for h in range(NH):
                        i_ = V.bn_stats(gst[:, h, :], half(xc[a.par], h))
                    i_.then_inc(s_gstats, 1)
                if o:
                    low_z(0)
                if a:
                    dve.wait_ge(s_gstats, a.n + 1)
                if o:
                    low_z(1)
                if a:
                    V.bn_aggr(gmv[:], gst[:].rearrange("p a b -> p (a b)")).then_inc(s_gmv, 1)
                if w:
                    key_rest(w, T - 1)
                if v:
                    scale_rows(1)
                if w:
                    key_tokens(w, T - 1)
                if o:
                    dve.wait_ge(s_logit_ps, o.n + 1)
                    logits = ps_misc[:, 0:2 * T * E].rearrange("p (t e) -> p t e", e=2 * E)
                    V.tensor_tensor(lgp[:], logits[:, :, 0:E], rb[:], ALU.add).then_inc(s_lg, 1)
                    dve.wait_ge(s_lg, LOGITS * o.n + 1)
                    V.tensor_tensor(lg[:], logits[:, :, E:2 * E], lgp[:], ALU.add).then_inc(s_lg, 1)
                if a:
                    dve.wait_ge(s_gmean_ps, a.n + 1)
                    V.tensor_copy(gmean[:], ps_misc[:, 0:1]).then_inc(s_gmeanv, 1)
                    dve.wait_ge(s_gmeanv, GMEAN * a.n + 1)
                    V.tensor_tensor(gdev[:], gmv[:, 0:1], gmean[:], ALU.subtract).then_inc(s_gmeanv, 1)
                    dve.wait_ge(s_gmeanv, GMEAN * a.n + 2)
                    V.scalar_tensor_tensor(out=gv[:], in0=gdev[:], scalar=gdev[:], in1=gmv[:, 1:2],
                                           op0=ALU.mult, op1=ALU.add).then_inc(s_gmeanv, 1)
                if o:
                    two_largest()
                if v:
                    key_rest(v, 0)
                    scale_rows(2)
                if o:
                    gates()
                if a:
                    dve.wait_ge(s_gvar_ps, a.n + 1)
                    V.tensor_scalar(gve[:], ps_misc[:, 0:1], GN_EPS, None, ALU.add).then_inc(s_gve, 1)
                if o:
                    gate_experts(o, 0)
                if v:
                    key_tokens(v, 0)
                if b:
                    conv_out(1)
                if v:
                    key_rest(v, 1)
                    scale_rows(3)
                if w:
                    attention_residual(0)
                if o:
                    gate_experts(o, 1)
                if v:
                    key_tokens(v, 1)
                if o:
                    gated_bias(0)
                if a:
                    dve.wait_ge(s_grs, a.n + 1)
                    if o:
                        dve.wait_ge(s_z_ps, NH * o.n + NH)
                    V.tensor_scalar(gnf, xc[a.par][:], gmean[:], grs[:], ALU.subtract, ALU.mult).then_inc(s_gnf, 1)
                if o:
                    gated_bias(1)
                if w:
                    attention_stats(0)
                if v:
                    key_rest(v, 2)
                    scale_rows(4)
                if w:
                    attention_residual(1)
                if o:
                    gate_experts(o, 2)
                if v:
                    key_tokens(v, 2)
                if w:
                    attention_stats(1)
                if a:
                    dve.wait_ge(s_gnhi, a.n + 1)
                    V.tensor_tensor(gnlo[:, 1:1 + H, 1:1 + W], rows(gnf),
                                    gnhi[:, 1:1 + H, 1:1 + W].bitcast(F32), ALU.subtract).then_inc(s_gnlo, 1)
                if b:
                    first_stats(0)
                    first_stats(1)
                    first_norms()
                if v:
                    key_rest(v, 3)
                    scale_rows(5)
                if o:
                    gate_experts(o, 3)
                if v:
                    key_tokens(v, 3)
                if w:
                    residual_norm(0)
                if v:
                    key_rest(v, 4)
                    scale_rows(6)
                if o:
                    gate_experts(o, 4)
                if v:
                    key_tokens(v, 4)
                if w:
                    residual_norm(1)
                if v:
                    key_rest(v, 5)
                    scale_rows(7)
                if o:
                    gate_experts(o, 5)
                if v:
                    key_tokens(v, 5)
                if b:
                    low_xn(0)
                if o:
                    gate_experts(o, 6)
                if b:
                    low_xn(1)

            iterations(dve, NB, run)


def kernel(x, L0_conv_weight, L0_conv_bias, L1_attn_ln_weight, L1_attn_ln_bias,
           L1_ffn_router_w, L1_ffn_router_b, L1_ffn_expert_w, L1_ffn_expert_b):
    import numpy as np
    import concourse.bacc as bacc
    from concourse.bass_utils import run_bass_kernel_spmd

    x = np.asarray(x)
    nb, c, h, w = x.shape
    tiles = h * w // P
    experts = L1_ffn_expert_b.shape[0]
    conv_weight, expert_weight = np.asarray(L0_conv_weight), np.asarray(L1_ffn_expert_w)
    group = c // 32
    same_group = np.arange(c)[:, None] // group == np.arange(c)[None, :] // group
    bias_rows = np.zeros((3 * experts, 2), np.float32)
    bias_rows[:2 * experts, 0] = 1
    bias_rows[2 * experts:, 1] = 1
    arrays = {
        "x": x.reshape(nb, c, h * w),
        "conv_w": conv_weight.transpose(1, 2, 3, 0).reshape(c, -1),
        "conv_b": np.asarray(L0_conv_bias).reshape(c, 1),
        "ln_w": np.broadcast_to(np.asarray(L1_attn_ln_weight), (P, c)),
        "ln_b": np.broadcast_to(np.asarray(L1_attn_ln_bias), (P, c)),
        "router_w": np.asarray(L1_ffn_router_w),
        "router_b": np.broadcast_to(np.asarray(L1_ffn_router_b), (P, tiles, experts)),
        "expert_w": expert_weight.transpose(1, 0, 2).reshape(c, -1),
        "expert_b": np.concatenate([np.asarray(L1_ffn_expert_b)] * 3),
        "identity": np.eye(P, dtype=np.float32),
        "group_mean": same_group.astype(np.float32) / np.float32(group),
        "expert_ids": np.broadcast_to(np.arange(experts, dtype=np.float32), (P, tiles, experts)),
        "bias_rows": bias_rows,
    }
    arrays = {k: np.ascontiguousarray(a) for k, a in arrays.items()}
    nc = bacc.Bacc("TRN2", target_bir_lowering=False, num_devices=1)
    aps = {k: nc.dram_tensor(k, a.shape, F32, kind="ExternalInput").ap() for k, a in arrays.items()}
    out = nc.dram_tensor("out", (nb, c, h * w), F32, kind="ExternalOutput").ap()
    build(nc, out=out, **aps)
    result = run_bass_kernel_spmd(nc, [arrays], core_ids=[0])
    return result.results[0]["out"].reshape(nb, c, h, w)
```

```python
from contextlib import ExitStack

import concourse.bass as bass
from concourse import mybir

F32 = mybir.dt.float32
F32R = mybir.dt.float32r
U32 = mybir.dt.uint32
ALU = mybir.AluOpType
ACT = mybir.ActivationFunctionType

P = 128
KS = 3
HALF = 512
GN_EPS, LNT_EPS, ATTN_EPS = 1e-5, 1e-5, 1e-6
SCALE, INV_TEMP = 0.1, 2.0
FIRST, STAGES_AHEAD, STAGES_BEHIND = -3, 3, 4


class Image:

    def __init__(self, pair, c):
        self.n = 2 * pair + c
        self.nth = pair + c // 2
        self.par = c % 2


class Iteration:

    def __init__(self, pair, c, images):
        self.pair, self.c, self.images = pair, c, images
        self.static = isinstance(pair, int)

    def image(self, d):
        if self.static and not 0 <= 2 * self.pair + self.c + d < self.images:
            return None
        return Image(self.pair, self.c + d)


def iterations(eng, images, run):
    last = images + STAGES_BEHIND
    begin = STAGES_BEHIND + 1
    pairs = (images - STAGES_AHEAD - begin) // 2
    for i in range(FIRST, begin):
        run(Iteration(0, i, images))
    with eng.Fori(0, pairs) as pair:
        run(Iteration(pair, begin, images))
        run(Iteration(pair, begin + 1, images))
    for i in range(begin + 2 * pairs, last):
        run(Iteration(0, i, images))


def build(nc, x, conv_w, conv_b, ln_w, ln_b, router_w, router_b, expert_w, expert_b,
          identity, group_mean, expert_ids, bias_rows, out):
    NB, C, HW = x.shape
    W = 32
    H = HW // W
    PW = W + 2
    T = HW // P
    NH = HW // HALF
    TPH = T // NH
    RPH = H // NH
    E = router_w.shape[1]
    TAPS = KS * KS
    STEPS = T

    with ExitStack() as ctx:
        def sb(name, shape, dt=F32):
            return ctx.enter_context(nc.sbuf_tensor(name, shape, dt))

        def psum(name, n=HALF):
            return ctx.enter_context(nc.psum_tensor(name, [P, n], F32))

        def sem(name):
            return ctx.enter_context(nc.semaphore(name))

        ident = sb("ident", [P, P])
        gmat = sb("gmat", [P, P])
        ids = sb("ids", [P, T, E])
        rows24 = sb("rows24", [3 * E, 2])
        cb = sb("cb", [P, 1])
        lnw = sb("lnw", [P, C])
        lnb = sb("lnb", [P, C])
        rb = sb("rb", [P, T, E])
        eb = sb("eb", [3 * E, C])
        ebt = sb("ebt", [3 * E, C])
        eblo = sb("eblo", [3 * E, C])
        ebhi = sb("ebhi", [3 * E, C], F32R)
        ebs = sb("ebs", [3 * E, C], F32R)
        rw = sb("rw", [P, E])
        rwhl = sb("rwhl", [P, 2 * E], F32R)
        rwhi, rwlo = rwhl[:, 0:E], rwhl[:, E:2 * E]
        cwhi = sb("cwhi", [P, TAPS, C], F32R)
        cwlo = sb("cwlo", [P, TAPS, C], F32R)
        ewhi = sb("ewhi", [P, E * C], F32R)
        ewlo = sb("ewlo", [P, E * C], F32R)
        nhalf = sb("nhalf", [P, 1])
        ones = sb("ones", [P, 1])
        xc = [sb(f"xc_{p}", [P, HW]) for p in range(2)]
        gst = sb("gst", [P, NH, 6])
        gmv = sb("gmv", [P, 2])
        gmean = sb("gmean", [P, 1])
        gdev = sb("gdev", [P, 1])
        gv = sb("gv", [P, 1])
        gve = sb("gve", [P, 1])
        grs = sb("grs", [P, 1])
        gnhi = sb("gnhi", [P, H + 2, PW], F32R)
        gnlo = sb("gnlo", [P, H + 2, PW], F32R)
        x1c = sb("x1c", [P, HW])
        x1t = [sb(f"x1t_{p}", [P, T, C]) for p in range(2)]
        l1st = sb("l1st", [P, T, 6])
        l1mv = [sb(f"l1mv_{p}", [P, T, 2]) for p in range(2)]
        l1ve = sb("l1ve", [P, T])
        l1rs = [sb(f"l1rs_{p}", [P, T]) for p in range(2)]
        l1rec = sb("l1rec", [P, T])
        l1q = sb("l1q", [P, T])
        l1nm = sb("l1nm", [P, T])
        l1n = sb("l1n", [P, T])
        l1in = sb("l1in", [P, T])
        l1a = sb("l1a", [P, T])
        l1nbn = sb("l1nbn", [P, T])
        l1nbu = [sb(f"l1nbu_{p}", [P, T]) for p in range(2)]
        xnhi = [sb(f"xnhi_{p}", [P, HW], F32R) for p in range(2)]
        xnlo = [sb(f"xnlo_{p}", [P, HW], F32R) for p in range(2)]
        es = sb("es", [P, T, HW])
        rsum = [sb(f"rsum_{p}", [P, T]) for p in range(2)]
        rinv = sb("rinv", [P, T])
        rbc = sb("rbc", [P, HW])
        s1 = [sb(f"s1_{p}", [P, HW]) for p in range(2)]
        s1hi = [sb(f"s1hi_{p}", [P, HW], F32R) for p in range(2)]
        s1lo = [sb(f"s1lo_{p}", [P, HW], F32R) for p in range(2)]
        fx = [sb(f"fx_{p}", [P, HW]) for p in range(2)]
        gx = [sb(f"gx_{p}", [P, HW], F32R) for p in range(2)]
        csum = [sb(f"csum_{p}", [P, T]) for p in range(2)]
        ci = [sb(f"ci_{p}", [P, T]) for p in range(2)]
        u = [sb(f"u_{p}", [P, T, C]) for p in range(2)]
        uhi = [sb(f"uhi_{p}", [P, C], F32R) for p in range(2)]
        ulo = [sb(f"ulo_{p}", [P, C], F32R) for p in range(2)]
        yhi = [sb(f"yhi_{p}", [P, C], F32R) for p in range(2)]
        x1b = [sb(f"x1b_{p}", [P, T, C]) for p in range(2)]
        y_part = sb("y_part", [P, C])
        ysum = sb("ysum", [P, 1])
        xneg = sb("xneg", [P, HW])
        yv = sb("yv", [P, T, C])
        outc = yv[:].rearrange("p t c -> p (t c)")
        l2st = sb("l2st", [P, T, 6])
        l2mv = sb("l2mv", [P, T, 2])
        l2ve = sb("l2ve", [P, T])
        l2rs = sb("l2rs", [P, T])
        t1 = [sb(f"t1_{p}", [P, T, C]) for p in range(2)]
        l3st = sb("l3st", [P, T, 6])
        l3mv = sb("l3mv", [P, T, 2])
        l3ve = sb("l3ve", [P, T])
        l3rs = sb("l3rs", [P, T])
        l3nm = sb("l3nm", [P, T])
        l3nb = sb("l3nb", [P, T])
        zt = sb("zt", [P, T, C])
        gnf = zt[:].rearrange("p t c -> p (t c)")
        xnt = zt
        zhi = sb("zhi", [P, HW], F32R)
        zlo = sb("zlo", [P, HW], F32R)
        lgp = sb("lgp", [P, T, E])
        lg = sb("lg", [P, T, E])
        mx = sb("mx", [P, T, 8])
        mi = sb("mi", [P, T, 8], U32)
        mf = sb("mf", [P, 2, T])
        gd = sb("gd", [P, T])
        ge = sb("ge", [P, T])
        gs = sb("gs", [P, T])
        g1 = sb("g1", [P, T])
        g2 = sb("g2", [P, T])
        gm1 = sb("gm1", [P, T, E])
        gm2 = sb("gm2", [P, T, E])
        gate = sb("gate", [P, T, E])
        g24 = sb("g24", [P, T, 3 * E], F32R)
        g24t = sb("g24t", [3 * E, HW], F32R)
        prod = [sb(f"prod_{p}", [P, E * C]) for p in range(2)]

        ps_conv = psum("ps_conv")
        ps_sim = psum("ps_sim", HW)
        ps_att = psum("ps_att", HW)
        ps_ffn = psum("ps_ffn", E * C)
        ps_misc = psum("ps_misc")

        s_const = sem("s_const")
        s_wsplit = sem("s_wsplit")
        s_gnpad = sem("s_gnpad")
        s_nhalf = sem("s_nhalf")
        s_ones = sem("s_ones")
        s_gstats = sem("s_gstats")
        s_gmv = sem("s_gmv")
        s_gmean_ps = sem("s_gmean_ps")
        s_gmeanv = sem("s_gmeanv")
        s_gvar_ps = sem("s_gvar_ps")
        s_gve = sem("s_gve")
        s_grs = sem("s_grs")
        s_gnf = sem("s_gnf")
        s_gnhi = sem("s_gnhi")
        s_gnlo = sem("s_gnlo")
        s_conv_ps = sem("s_conv_ps")
        s_x1c = sem("s_x1c")
        s_x1t_ps = sem("s_x1t_ps")
        s_x1t = sem("s_x1t")
        s_l1st = sem("s_l1st")
        s_l1mv = sem("s_l1mv")
        s_l1ve = sem("s_l1ve")
        s_l1rs = sem("s_l1rs")
        s_l1q = sem("s_l1q")
        s_l1n = sem("s_l1n")
        s_l1a = sem("s_l1a")
        s_xnt = sem("s_xnt")
        s_xn_ps = sem("s_xn_ps")
        s_xnhi = sem("s_xnhi")
        s_xnlo = sem("s_xnlo")
        s_sim_ps = sem("s_sim_ps")
        s_e_tile = sem("s_e_tile")
        s_rinv = sem("s_rinv")
        s_rb_ps = sem("s_rb_ps")
        s_rb = sem("s_rb")
        s_s_tile = sem("s_s_tile")
        s_f_tile = sem("s_f_tile")
        s_s_hi = sem("s_s_hi")
        s_s_lo = sem("s_s_lo")
        s_ci = sem("s_ci")
        s_u_hi = sem("s_u_hi")
        s_y_hi = sem("s_y_hi")
        s_u_lo = sem("s_u_lo")
        s_g_tile = sem("s_g_tile")
        s_att_ps = sem("s_att_ps")
        s_u_tokens = sem("s_u_tokens")
        s_x1b = sem("s_x1b")
        s_y_part = sem("s_y_part")
        s_ysum_ps = sem("s_ysum_ps")
        s_ysum = sem("s_ysum")
        s_xneg = sem("s_xneg")
        s_xnegt_ps = sem("s_xnegt_ps")
        s_yv = sem("s_yv")
        s_l2st = sem("s_l2st")
        s_l2mv = sem("s_l2mv")
        s_l2ve = sem("s_l2ve")
        s_l2rs = sem("s_l2rs")
        s_l2q = sem("s_l2q")
        s_t1 = sem("s_t1")
        s_l3st = sem("s_l3st")
        s_l3mv = sem("s_l3mv")
        s_l3ve = sem("s_l3ve")
        s_l3rs = sem("s_l3rs")
        s_l3nb = sem("s_l3nb")
        s_z_tokens = sem("s_z_tokens")
        s_z_ps = sem("s_z_ps")
        s_zhi = sem("s_zhi")
        s_zlo = sem("s_zlo")
        s_logit_ps = sem("s_logit_ps")
        s_lg = sem("s_lg")
        s_mx = sem("s_mx")
        s_mi = sem("s_mi")
        s_gd = sem("s_gd")
        s_ge = sem("s_ge")
        s_gate = sem("s_gate")
        s_gate24 = sem("s_gate24")
        s_gt_ps = sem("s_gt_ps")
        s_gt = sem("s_gt")
        s_gb_ps = sem("s_gb_ps")
        s_t1b = sem("s_t1b")
        s_ffn_ps = sem("s_ffn_ps")
        s_prod = sem("s_prod")
        s_tree = sem("s_tree")
        s_t2 = sem("s_t2")
        s_out_ps = sem("s_out_ps")
        s_outc = sem("s_outc")
        s_stored = [sem(f"s_stored{h}") for h in range(NH)]
        s_loaded = [sem(f"s_loaded{p}") for p in range(2)]

        block = ctx.enter_context(nc.Block())

        def half(ap, h):
            return ap[:, h * HALF:(h + 1) * HALF]

        def tile(ap, t):
            return ap[:, t * P:(t + 1) * P]

        def half_t(ap, h):
            return ap[:, h * TPH:(h + 1) * TPH, :]

        def padded(ap, h, dy=1, dx=1):
            return ap[:, h * RPH + dy:h * RPH + dy + RPH, dx:dx + W]

        def rows(ap):
            return ap.rearrange("p (r w) -> p r w", w=W)

        CONST_LOADS = 12
        WSPLIT = 10
        GMEAN, GATE, FIRST_SCALES, L3, LOGITS = 3, 10, 3, 2, 2
        TREE = 3

        def count(value):
            return max(value, 0) if isinstance(value, int) else value

        def dram(ap, it, image):
            return ap[image.n] if it.static else ap[bass.ds(image.n, 1)].rearrange("a p n -> (a p) n")

        @block.sync
        def _(sp):
            es_flat = es[:].rearrange("p t n -> p (t n)")
            loads = [(ident[:], identity), (gmat[:], group_mean), (ids[:], expert_ids), (rows24[:], bias_rows),
                     (cb[:], conv_b), (lnw[:], ln_w), (lnb[:], ln_b), (rb[:], router_b), (eb[:], expert_b),
                     (rw[:], router_w), (es_flat[:, 0:TAPS * C], conv_w),
                     (es_flat[:, TAPS * C:TAPS * C + E * C], expert_w)]
            sp.dma_start(xc[0][:], x[0]).then_inc(s_loaded[0], 16)
            for dst, src in loads:
                sp.dma_start(dst, src).then_inc(s_const, 16)

            def run(it):
                q, ahead = it.image(-4), it.image(3)
                if ahead and not (it.static and ahead.n == 0):
                    sp.wait_ge(s_x1c, count(NH * (ahead.n - 2) + NH))
                    sp.dma_start(xc[ahead.par][:], dram(x, it, ahead)).then_inc(s_loaded[ahead.par], 16)
                if q:
                    for h in range(NH):
                        sp.wait_ge(s_outc, NH * q.n + h + 1)
                        sp.dma_start(half(dram(out, it, q), h), half(outc, h)).then_inc(s_stored[h], 16)

            iterations(sp, NB, run)
            for h in range(NH):
                sp.wait_ge(s_stored[h], 16 * NB)

        @block.tensor
        def _(pe):
            pe.wait_ge(s_const, 16 * CONST_LOADS)
            pe.wait_ge(s_wsplit, WSPLIT)
            pe.wait_ge(s_ones, 1)
            mm = nc.tensor.matmul
            PARTS = 3

            def run(it):
                ahead, a, b, c, v, w, o, q = (it.image(d) for d in (3, 2, 1, 0, -1, -2, -3, -4))

                if c:
                    reader = (s_xnlo, NH * c.n + NH)
                elif o:
                    reader = (s_yv, NH * o.n + NH)
                elif q:
                    reader = (s_t1b, NH * q.n + NH)
                elif b:
                    reader = (s_gve, b.n + 1)
                else:
                    reader = (s_gve, 0)

                def sim(t):
                    pe.wait_ge(s_xnlo, NH * c.n + NH)
                    pe.wait_ge(s_e_tile, T * c.n + t)
                    hi, lo = xnhi[c.par], xnlo[c.par]
                    for h in range(NH):
                        mm(half(ps_sim, h), tile(hi, t), half(hi, h), start=True, stop=False)
                        mm(half(ps_sim, h), tile(hi, t), half(lo, h), start=False, stop=False)
                        m = mm(half(ps_sim, h), tile(lo, t), half(hi, h), start=False, stop=True)
                    m.then_inc(s_sim_ps, 1)

                def conv(g, h, first, last):
                    for n in range(first, last):
                        tap, part = divmod(n, PARTS)
                        if n == 0:
                            pe.wait_ge(s_gnhi, g.n + 1)
                            pe.wait_ge(s_gnlo, g.n + 1)
                            pe.wait_ge(s_x1c, NH * g.n + h)
                        wts, src = ((cwhi, gnhi), (cwhi, gnlo), (cwlo, gnhi))[part]
                        m = mm(rows(ps_conv[:]), wts[:, tap, :], padded(src, h, tap // KS, tap % KS),
                               start=(n == 0), stop=(n == TAPS * PARTS - 1))
                        if n == TAPS * PARTS - 1:
                            m.then_inc(s_conv_ps, 1)

                def attend(g, k):
                    pe.wait_ge(s_s_hi, T * g.n + k + 1)
                    pe.wait_ge(s_s_lo, T * g.n + k + 1)
                    pe.wait_ge(s_u_lo, T * g.n + k + 1)
                    pe.wait_ge(s_y_hi, T * g.n + k + 1)
                    pe.wait_ge(s_g_tile, T * g.n + k + 1)
                    if k == 0:
                        pe.wait_ge(s_xneg, NH * g.n)
                    r = k % 2
                    for h in range(NH):
                        mm(half(ps_att, h), uhi[r][:], half(s1hi[r], h), start=(k == 0), stop=False)
                        mm(half(ps_att, h), uhi[r][:], half(s1lo[r], h), start=False, stop=False)
                        mm(half(ps_att, h), ulo[r][:], half(s1hi[r], h), start=False, stop=False)
                        m = mm(half(ps_att, h), yhi[r][:], half(gx[r], h), start=False, stop=(k == T - 1))
                    m.then_inc(s_att_ps, 1)

                def ffn(g, t):
                    pe.wait_ge(s_zlo, NH * g.n + NH)
                    pe.wait_ge(s_prod, T * g.n + t)
                    for h in range(NH):
                        mm(half(ps_ffn, h), tile(zhi, t), half(ewhi, h), start=True, stop=False)
                        mm(half(ps_ffn, h), tile(zhi, t), half(ewlo, h), start=False, stop=False)
                        m = mm(half(ps_ffn, h), tile(zlo, t), half(ewhi, h), start=False, stop=True)
                    m.then_inc(s_ffn_ps, 1)

                def transposes(src_tile, h):
                    for j in range(TPH):
                        m = nc.tensor.transpose(tile(ps_misc, j), src_tile(h * TPH + j), ident[:])
                    return m

                def misc_rb(h):
                    nonlocal reader
                    pe.wait_ge(s_rinv, v.n + 1)
                    pe.wait_ge(*reader)
                    reader = (s_rb, NH * v.n + h + 1)
                    transposes(lambda t: rinv[:, t:t + 1].to_broadcast([P, P]), h).then_inc(s_rb_ps, 1)

                def misc_ysum():
                    nonlocal reader
                    pe.wait_ge(s_y_part, T * w.n + T)
                    pe.wait_ge(*reader)
                    reader = (s_ysum, w.n + 1)
                    mm(ps_misc[:, 0:1], y_part[:], ones[:], start=True, stop=True).then_inc(s_ysum_ps, 1)

                def misc_out(h):
                    nonlocal reader
                    pe.wait_ge(s_t2, T * q.n + (h + 1) * TPH)
                    pe.wait_ge(*reader)
                    reader = (s_outc, NH * q.n + h + 1)
                    transposes(lambda t: t1[q.par][:, t, :], h).then_inc(s_out_ps, 1)

                def misc_xneg(h):
                    nonlocal reader
                    pe.wait_ge(s_xneg, NH * w.n + h + 1)
                    pe.wait_ge(*reader)
                    reader = (s_yv, NH * w.n + h + 1)
                    transposes(lambda t: tile(xneg, t), h).then_inc(s_xnegt_ps, 1)

                def misc_z(h):
                    nonlocal reader
                    pe.wait_ge(s_z_tokens, NH * o.n + h + 1)
                    pe.wait_ge(*reader)
                    reader = (s_zlo, NH * o.n + h + 1)
                    transposes(lambda t: zt[:, t, :], h).then_inc(s_z_ps, 1)

                def router(first, last):
                    for t in range(first, last):
                        at = 2 * E * t
                        mm(ps_misc[:, at:at + 2 * E], tile(zhi, t), rwhl[:], start=True, stop=False)
                        m = mm(ps_misc[:, at:at + E], tile(zlo, t), rwhi, start=False, stop=True)
                    return m

                def misc_router():
                    nonlocal reader
                    pe.wait_ge(s_zlo, NH * o.n + NH)
                    pe.wait_ge(*reader)
                    reader = (s_lg, LOGITS * o.n + LOGITS)
                    router(0, 3)

                def misc_gmean():
                    nonlocal reader
                    pe.wait_ge(s_gmv, a.n + 1)
                    pe.wait_ge(*reader)
                    reader = (s_gmeanv, GMEAN * a.n + 1)
                    mm(ps_misc[:, 0:1], gmat[:], gmv[:, 0:1], start=True, stop=True).then_inc(s_gmean_ps, 1)

                def misc_gvar():
                    nonlocal reader
                    pe.wait_ge(s_gmeanv, GMEAN * a.n + GMEAN)
                    pe.wait_ge(*reader)
                    reader = (s_gve, a.n + 1)
                    mm(ps_misc[:, 0:1], gmat[:], gv[:], start=True, stop=True).then_inc(s_gvar_ps, 1)

                def misc_x1(h):
                    nonlocal reader
                    pe.wait_ge(s_x1c, NH * b.n + h + 1)
                    pe.wait_ge(*reader)
                    reader = (s_x1t, NH * b.n + h + 1)
                    transposes(lambda t: tile(x1c, t), h).then_inc(s_x1t_ps, 1)

                def misc_gt(h):
                    nonlocal reader
                    pe.wait_ge(s_gate24, o.n + 1)
                    pe.wait_ge(*reader)
                    reader = (s_gt, NH * o.n + h + 1)
                    for j in range(TPH):
                        m = nc.tensor.transpose(tile(ps_misc, j)[0:3 * E, :],
                                                g24[:, h * TPH + j, :].bitcast(F32), ident[:])
                    m.then_inc(s_gt_ps, 1)

                def misc_gb(h):
                    nonlocal reader
                    pe.wait_ge(s_gt, NH * o.n + h + 1)
                    pe.wait_ge(*reader)
                    reader = (s_t1b, NH * o.n + h + 1)
                    for j in range(TPH):
                        m = mm(tile(ps_misc, j), tile(g24t, h * TPH + j), ebs[:], start=True, stop=True)
                    m.then_inc(s_gb_ps, 1)

                def misc_xn(h):
                    nonlocal reader
                    pe.wait_ge(s_xnt, NH * b.n + h + 1)
                    pe.wait_ge(*reader)
                    reader = (s_xnlo, NH * b.n + h + 1)
                    transposes(lambda t: xnt[:, t, :], h).then_inc(s_xn_ps, 1)

                if a:
                    misc_gmean()
                if v:
                    misc_rb(0)
                if b:
                    conv(b, 1, 21, 27)
                if v:
                    misc_rb(1)
                if q:
                    ffn(q, T - 1)
                if o:
                    misc_z(0)
                if c:
                    sim(0)
                if o:
                    misc_z(1)
                if w:
                    attend(w, T - 2)
                if o:
                    misc_router()
                    router(3, 6)
                    router(6, T).then_inc(s_logit_ps, 1)
                if c:
                    sim(1)
                if b:
                    misc_x1(0)
                if w:
                    attend(w, T - 1)
                if b:
                    misc_x1(1)
                if o:
                    ffn(o, 0)
                if a:
                    misc_gvar()
                if w:
                    misc_ysum()
                if q:
                    misc_out(0)
                if c:
                    sim(2)
                if o:
                    misc_gt(0)
                if v:
                    attend(v, 0)
                if o:
                    misc_gb(0)
                    ffn(o, 1)
                    misc_gt(1)
                if c:
                    sim(3)
                if w:
                    misc_xneg(0)
                if v:
                    attend(v, 1)
                if q:
                    misc_out(1)
                if a:
                    conv(a, 0, 0, 9)
                if o:
                    misc_gb(1)
                    ffn(o, 2)
                if w:
                    misc_xneg(1)
                if a:
                    conv(a, 0, 9, 21)
                if v:
                    attend(v, 2)
                if c:
                    sim(4)
                if a:
                    conv(a, 0, 21, 27)
                if b:
                    misc_xn(0)
                if o:
                    ffn(o, 3)
                if v:
                    attend(v, 3)
                if c:
                    sim(5)
                if a:
                    conv(a, 1, 0, 12)
                if o:
                    ffn(o, 4)
                if v:
                    attend(v, 4)
                if c:
                    sim(6)
                if b:
                    misc_xn(1)
                if a:
                    conv(a, 1, 12, 21)
                if c:
                    sim(7)
                if o:
                    ffn(o, 5)
                if v:
                    attend(v, 5)
                if o:
                    ffn(o, 6)

            iterations(pe, NB, run)

        @block.scalar
        def _(act):
            act.wait_ge(s_gnpad, 2)
            act.wait_ge(s_wsplit, WSPLIT)

            def run(it):
                ahead, a, b, c, v, w, o, q = (it.image(d) for d in (3, 2, 1, 0, -1, -2, -3, -4))

                def exp_sim(t):
                    act.wait_ge(s_sim_ps, T * c.n + t + 1)
                    if v:
                        act.wait_ge(s_s_tile, T * v.n + t + 1)
                    nc.scalar.activation(es[:, t, :], ps_sim[:], ACT.Exp, scale=INV_TEMP,
                                         accum_out=rsum[c.par][:, t:t + 1]).then_inc(s_e_tile, 1)

                def exp_s(g, t):
                    act.wait_ge(s_s_tile, T * g.n + t + 1)
                    act.wait_ge(s_g_tile, count(T * g.n + t - 1))
                    nc.scalar.activation(fx[t % 2][:], s1[t % 2][:], ACT.Exp,
                                         accum_out=csum[g.par][:, t:t + 1]).then_inc(s_f_tile, 1)

                def round_s(g, t):
                    act.wait_ge(s_att_ps, count(T * g.n + t - 1))
                    nc.scalar.copy(s1hi[t % 2][:], s1[t % 2][:]).then_inc(s_s_hi, 1)

                def round_u_and_y(g, k):
                    r = k % 2
                    n = T * g.n + k
                    act.wait_ge(s_u_tokens, g.n + 1)
                    act.wait_ge(s_att_ps, count(n - 1))
                    nc.scalar.copy(uhi[r][:], u[g.par][:, k, :]).then_inc(s_u_hi, 1)
                    act.wait_ge(s_ci, n + 1)
                    nc.scalar.activation(yhi[r][:], u[g.par][:, k, :], ACT.Identity,
                                         scale=ci[g.par][:, k:k + 1]).then_inc(s_y_hi, 1)

                def rb_copy(h):
                    act.wait_ge(s_rb_ps, NH * v.n + h + 1)
                    act.wait_ge(s_s_tile, T * v.n)
                    nc.scalar.copy(half(rbc, h), ps_misc[:]).then_inc(s_rb, 1)

                def ysum_copy():
                    act.wait_ge(s_ysum_ps, w.n + 1)
                    act.wait_ge(s_xneg, NH * w.n)
                    nc.scalar.copy(ysum[:], ps_misc[:, 0:1]).then_inc(s_ysum, 1)

                def xneg_copy(h):
                    act.wait_ge(s_ysum, w.n + 1)
                    act.wait_ge(s_att_ps, T * w.n + T)
                    act.wait_ge(s_xnegt_ps, NH * w.n)
                    nc.scalar.activation(half(xneg, h), half(ps_att, h), ACT.Identity,
                                         bias=ysum[:]).then_inc(s_xneg, 1)

                def out_copy(h):
                    act.wait_ge(s_out_ps, NH * q.n + h + 1)
                    act.wait_ge(s_stored[h], 16 * q.n)
                    nc.scalar.copy(half(outc, h), ps_misc[:]).then_inc(s_outc, 1)

                def x1_copy(h):
                    act.wait_ge(s_x1t_ps, NH * b.n + h + 1)
                    act.wait_ge(s_x1b, count(b.n - 1))
                    act.wait_ge(s_u_tokens, count(b.n - 1))
                    nc.scalar.copy(half(x1t[b.par][:].rearrange("p t c -> p (t c)"), h), ps_misc[:]).then_inc(s_x1t, 1)

                def z_round(h):
                    act.wait_ge(s_z_ps, NH * o.n + h + 1)
                    act.wait_ge(s_ffn_ps, T * o.n)
                    nc.scalar.copy(half(zhi, h), ps_misc[:]).then_inc(s_zhi, 1)

                def gate_copy(h):
                    act.wait_ge(s_gt_ps, NH * o.n + h + 1)
                    act.wait_ge(s_gb_ps, NH * o.n)
                    nc.scalar.copy(half(g24t, h), ps_misc[0:3 * E, :]).then_inc(s_gt, 1)

                def xn_round(h):
                    act.wait_ge(s_xn_ps, NH * b.n + h + 1)
                    act.wait_ge(s_sim_ps, count(T * (b.n - 1)))
                    nc.scalar.copy(half(xnhi[b.par], h), ps_misc[:]).then_inc(s_xnhi, 1)

                def unit_tokens():
                    act.wait_ge(s_x1t, NH * c.n + NH)
                    act.wait_ge(s_l1a, FIRST_SCALES * c.n + FIRST_SCALES)
                    act.wait_ge(s_yv, count(NH * (c.n - 2) + NH))
                    act.wait_ge(s_ysum_ps, count(c.n - 1))
                    for t in range(T):
                        i_ = nc.scalar.activation(u[c.par][:, t, :], x1t[c.par][:, t, :], ACT.Identity,
                                                  scale=l1rs[c.par][:, t:t + 1], bias=l1nbu[c.par][:, t:t + 1])
                    i_.then_inc(s_u_tokens, 1)

                def normalise(h):
                    act.wait_ge(s_l1a, FIRST_SCALES * b.n + FIRST_SCALES)
                    act.wait_ge(s_x1t, NH * b.n + NH)
                    act.wait_ge(s_xn_ps, NH * b.n)
                    if o:
                        act.wait_ge(s_z_ps, NH * o.n + NH)
                    if a:
                        act.wait_ge(s_gnlo, a.n + 1)
                    for t in range(h * TPH, (h + 1) * TPH):
                        i_ = nc.scalar.activation(xnt[:, t, :], x1t[b.par][:, t, :], ACT.Identity,
                                                  scale=l1a[:, t:t + 1], bias=l1nbn[:, t:t + 1])
                    i_.then_inc(s_xnt, 1)

                def z_tokens(g, h):
                    act.wait_ge(s_l3nb, g.n + 1)
                    act.wait_ge(s_z_ps, NH * g.n)
                    if b and g is w:
                        act.wait_ge(s_xn_ps, NH * b.n + NH)
                    for t in range(h * TPH, (h + 1) * TPH):
                        i_ = nc.scalar.activation(zt[:, t, :], t1[g.par][:, t, :], ACT.Identity,
                                                  scale=l3rs[:, t:t + 1], bias=l3nb[:, t:t + 1])
                    i_.then_inc(s_z_tokens, 1)

                if o:
                    z_tokens(o, 1)
                if v:
                    rb_copy(0)
                if w:
                    round_u_and_y(w, T - 2)
                if v:
                    rb_copy(1)
                if w:
                    round_s(w, T - 1)
                if o:
                    z_round(0)
                if w:
                    round_u_and_y(w, T - 1)
                if v:
                    exp_s(v, 0)
                if o:
                    z_round(1)
                if c:
                    exp_sim(0)
                if v:
                    exp_s(v, 1)
                    round_u_and_y(v, 0)
                if o:
                    act.wait_ge(s_gd, o.n + 1)
                    nc.scalar.activation(ge[:], gd[:], ACT.Exp).then_inc(s_ge, 1)
                if b:
                    x1_copy(0)
                if c:
                    exp_sim(1)
                if v:
                    round_s(v, 0)
                if b:
                    x1_copy(1)
                if v:
                    round_s(v, 1)
                if w:
                    ysum_copy()
                    xneg_copy(0)
                if q:
                    out_copy(0)
                if w:
                    xneg_copy(1)
                if v:
                    exp_s(v, 2)
                if o:
                    gate_copy(0)
                if a:
                    act.wait_ge(s_gnf, a.n + 1)
                    if b:
                        act.wait_ge(s_conv_ps, NH * b.n + NH)
                    nc.scalar.copy(gnhi[:, 1:1 + H, 1:1 + W], rows(gnf)).then_inc(s_gnhi, 1)
                if c:
                    exp_sim(2)
                if v:
                    round_u_and_y(v, 1)
                if o:
                    gate_copy(1)
                if v:
                    round_s(v, 2)
                    exp_s(v, 3)
                if q:
                    out_copy(1)
                if v:
                    round_u_and_y(v, 2)
                    round_s(v, 3)
                if c:
                    exp_sim(3)
                if b:
                    normalise(0)
                if c:
                    unit_tokens()
                if v:
                    exp_s(v, 4)
                if b:
                    normalise(1)
                if v:
                    round_u_and_y(v, 3)
                if c:
                    exp_sim(4)
                if v:
                    round_s(v, 4)
                    round_s(v, 5)
                if c:
                    exp_sim(5)
                if b:
                    xn_round(0)
                if v:
                    round_u_and_y(v, 4)
                    round_s(v, 6)
                    exp_s(v, 5)
                if c:
                    exp_sim(6)
                if v:
                    round_u_and_y(v, 5)
                if b:
                    xn_round(1)
                if v:
                    exp_s(v, 6)
                    exp_s(v, 7)
                if c:
                    exp_sim(7)
                if w:
                    z_tokens(w, 0)

            iterations(act, NB, run)

        @block.gpsimd
        def _(pool):
            add = nc.gpsimd.tensor_tensor
            nc.gpsimd.memset(nhalf[:], -0.5).then_inc(s_nhalf, 1)
            nc.gpsimd.memset(ones[:], 1.0).then_inc(s_ones, 1)
            nc.gpsimd.memset(gnhi[:].bitcast(F32), 0.0).then_inc(s_gnpad, 1)
            nc.gpsimd.memset(gnlo[:].bitcast(F32), 0.0).then_inc(s_gnpad, 1)
            pool.wait_ge(s_nhalf, 1)
            pool.wait_ge(s_const, 16 * CONST_LOADS)

            def run(it):
                ahead, a, b, c, v, w, o, q = (it.image(d) for d in (3, 2, 1, 0, -1, -2, -3, -4))

                def inv_sqrt(dst, src):
                    return nc.gpsimd.tensor_tensor(dst, src, nhalf[:].to_broadcast([P, src.shape[1]]), ALU.pow)

                def low_s(g, t):
                    pool.wait_ge(s_s_hi, T * g.n + t + 1)
                    pool.wait_ge(s_att_ps, count(T * g.n + t - 1))
                    nc.gpsimd.tensor_tensor(s1lo[t % 2][:], s1[t % 2][:], s1hi[t % 2][:].bitcast(F32),
                                            ALU.subtract).then_inc(s_s_lo, 1)

                def expert_tree(g, t):
                    p = prod[t % 2]
                    pool.wait_ge(s_prod, T * g.n + t + 1)
                    for k in range(TREE):
                        n = E * C >> (k + 1)
                        add(p[:, 0:n], p[:, 0:n], p[:, n:2 * n], ALU.add).then_inc(s_tree, 1)
                        pool.wait_ge(s_tree, TREE * (T * g.n + t) + k + 1)

                def expert_add(g, t):
                    pool.wait_ge(s_t1b, NH * g.n + NH)
                    add(t1[g.par][:, t, :], t1[g.par][:, t, :], prod[t % 2][:, 0:C], ALU.add).then_inc(s_t2, 1)

                def first_scales():
                    pool.wait_ge(s_l1ve, b.n + 1)
                    pool.wait_ge(s_u_tokens, count(b.n - 1))
                    inv_sqrt(l1rs[b.par][:], l1ve[:]).then_inc(s_l1rs, 1)
                    pool.wait_ge(s_l1q, 3 * b.n + 3)
                    inv_sqrt(l1in[:], l1n[:]).then_inc(s_l1n, 1)
                    pool.wait_ge(s_l1rs, b.n + 1)
                    pool.wait_ge(s_l1n, b.n + 1)
                    pool.wait_ge(s_xnt, NH * b.n)
                    mul = nc.gpsimd.tensor_tensor
                    mul(l1a[:], l1rs[b.par][:], l1in[:], ALU.mult).then_inc(s_l1a, 1)
                    mul(l1nbu[b.par][:], l1nm[:], l1rs[b.par][:], ALU.mult).then_inc(s_l1a, 1)
                    pool.wait_ge(s_l1a, FIRST_SCALES * b.n + 1)
                    mul(l1nbn[:], l1nm[:], l1a[:], ALU.mult).then_inc(s_l1a, 1)

                if q:
                    expert_tree(q, T - 2)
                    expert_add(q, T - 2)
                if w:
                    low_s(w, T - 1)
                if v:
                    pool.wait_ge(s_x1t, NH * v.n + NH)
                    pool.wait_ge(s_t1, count(NH * (v.n - 2) + NH))
                    add(x1b[v.par][:], x1t[v.par][:], lnb[:].unsqueeze(1).to_broadcast([P, T, C]),
                        ALU.add).then_inc(s_x1b, 1)
                if q:
                    expert_tree(q, T - 1)
                if v:
                    low_s(v, 0)
                if a:
                    pool.wait_ge(s_gve, a.n + 1)
                    inv_sqrt(grs[:], gve[:]).then_inc(s_grs, 1)
                if v:
                    low_s(v, 1)
                if b:
                    first_scales()
                if q:
                    expert_add(q, T - 1)
                if o:
                    expert_tree(o, 0)
                if v:
                    low_s(v, 2)
                if o:
                    expert_add(o, 0)
                    expert_tree(o, 1)
                if v:
                    low_s(v, 3)
                if o:
                    expert_add(o, 1)
                if w:
                    pool.wait_ge(s_l2ve, w.n + 1)
                    inv_sqrt(l2rs[:], l2ve[:]).then_inc(s_l2rs, 1)
                if o:
                    expert_tree(o, 2)
                if v:
                    low_s(v, 4)
                if o:
                    expert_add(o, 2)
                if v:
                    low_s(v, 5)
                if o:
                    expert_tree(o, 3)
                    expert_add(o, 3)
                if v:
                    low_s(v, 6)
                if w:
                    pool.wait_ge(s_l3ve, L3 * w.n + L3)
                    pool.wait_ge(s_z_tokens, NH * w.n)
                    inv_sqrt(l3rs[:], l3ve[:]).then_inc(s_l3rs, 1)
                    pool.wait_ge(s_l3rs, w.n + 1)
                    nc.gpsimd.tensor_tensor(l3nb[:], l3nm[:], l3rs[:], ALU.mult).then_inc(s_l3nb, 1)
                if o:
                    expert_tree(o, 4)
                    expert_add(o, 4)
                    expert_tree(o, 5)
                    expert_add(o, 5)

            iterations(pool, NB, run)

        @block.vector
        def _(dve):
            V = nc.vector
            es_flat = es[:].rearrange("p t n -> p (t n)")
            dve.wait_ge(s_const, 16 * CONST_LOADS)
            cw = es_flat[:, 0:TAPS * C]
            ew = es_flat[:, TAPS * C:TAPS * C + E * C]
            cwh, cwl = (ap[:].rearrange("p a b -> p (a b)") for ap in (cwhi, cwlo))
            V.tensor_copy(cwh, cw).then_inc(s_wsplit, 1)
            V.tensor_copy(ewhi[:], ew).then_inc(s_wsplit, 1)
            V.tensor_copy(rwhi, rw[:]).then_inc(s_wsplit, 1)
            V.tensor_copy(ebhi[:], eb[:]).then_inc(s_wsplit, 1)
            dve.wait_ge(s_wsplit, 4)
            V.tensor_tensor(cwl, cw, cwh.bitcast(F32), ALU.subtract).then_inc(s_wsplit, 1)
            V.tensor_tensor(ewlo[:], ew, ewhi[:].bitcast(F32), ALU.subtract).then_inc(s_wsplit, 1)
            V.tensor_tensor(rwlo, rw[:], rwhi.bitcast(F32), ALU.subtract).then_inc(s_wsplit, 1)
            V.tensor_tensor(eblo[:], eb[:], ebhi[:].bitcast(F32), ALU.subtract).then_inc(s_wsplit, 1)
            dve.wait_ge(s_wsplit, 8)
            V.tensor_scalar(ebt[:], eblo[:], rows24[:, 1:2], None, ALU.mult).then_inc(s_wsplit, 1)
            dve.wait_ge(s_wsplit, 9)
            V.scalar_tensor_tensor(out=ebs[:], in0=ebhi[:].bitcast(F32), scalar=rows24[:, 0:1], in1=ebt[:],
                                   op0=ALU.mult, op1=ALU.add).then_inc(s_wsplit, 1)

            def run(it):
                ahead, a, b, c, v, w, o, q = (it.image(d) for d in (3, 2, 1, 0, -1, -2, -3, -4))

                def flat(ap, h):
                    return half_t(ap, h).rearrange("p t c -> p (t c)")

                def of_half(h):
                    return range(h * TPH, (h + 1) * TPH)

                def token_stats(src, st, mv, h, g, st_done, mv_done):
                    for t in of_half(h):
                        i_ = V.bn_stats(st[:, t, :], src[:, t, :])
                    i_.then_inc(st_done, 1)
                    dve.wait_ge(s_wsplit, 1)
                    dve.wait_ge(st_done, NH * g.n + h + 1)
                    for t in of_half(h):
                        i_ = V.bn_aggr(mv[:, t, :], st[:, t, :])
                    i_.then_inc(mv_done, 1)

                def scale_rows(k):
                    dve.wait_ge(s_rb, NH * v.n + NH)
                    dve.wait_ge(s_s_lo, count(T * v.n + k - 1))
                    dve.wait_ge(s_f_tile, count(T * v.n + k - 1))
                    V.tensor_tensor(s1[k % 2][:], es[:, k, :], rbc[:], ALU.mult).then_inc(s_s_tile, 1)

                def expm1_tile(g, k):
                    n = T * g.n + k
                    dve.wait_ge(s_f_tile, n + 1)
                    V.reciprocal(ci[g.par][:, k:k + 1], csum[g.par][:, k:k + 1]).then_inc(s_ci, 1)
                    dve.wait_ge(s_att_ps, count(n - 1))
                    V.tensor_scalar(gx[k % 2][:], fx[k % 2][:], -1.0, None, ALU.add).then_inc(s_g_tile, 1)

                def low_u(g, k):
                    r = k % 2
                    n = T * g.n + k
                    dve.wait_ge(s_u_hi, n + 1)
                    V.tensor_tensor(ulo[r][:], u[g.par][:, k, :], uhi[r][:].bitcast(F32),
                                    ALU.subtract).then_inc(s_u_lo, 1)

                def sum_key(g, k):
                    n = T * g.n + k
                    cik, uk = ci[g.par][:, k:k + 1], u[g.par][:, k, :]
                    dve.wait_ge(s_ci, n + 1)
                    dve.wait_ge(s_u_tokens, g.n + 1)
                    if k == 0:
                        dve.wait_ge(s_ysum_ps, g.n)
                        V.tensor_scalar(y_part[:], uk, cik, None, ALU.mult).then_inc(s_y_part, 1)
                    else:
                        dve.wait_ge(s_y_part, n)
                        V.scalar_tensor_tensor(out=y_part[:], in0=uk, scalar=cik, in1=y_part[:],
                                               op0=ALU.mult, op1=ALU.add).then_inc(s_y_part, 1)

                def attention_residual(h):
                    dve.wait_ge(s_xnegt_ps, NH * w.n + h + 1)
                    if q:
                        dve.wait_ge(s_stored[h], 16 * q.n + 16)
                    V.scalar_tensor_tensor(out=flat(yv, h), in0=ps_misc[:], scalar=-SCALE,
                                           in1=flat(u[w.par], h), op0=ALU.mult, op1=ALU.add).then_inc(s_yv, 1)

                def attention_stats(h):
                    dve.wait_ge(s_yv, NH * w.n + h + 1)
                    token_stats(yv, l2st, l2mv, h, w, s_l2st, s_l2mv)
                    if h == NH - 1:
                        dve.wait_ge(s_l2mv, NH * w.n + NH)
                        V.tensor_scalar(l2ve[:], l2mv[:, :, 1], ATTN_EPS, None, ALU.add).then_inc(s_l2ve, 1)

                def residual_norm(h):
                    dve.wait_ge(s_l2rs, w.n + 1)
                    dve.wait_ge(s_x1b, w.n + 1)
                    dve.wait_ge(s_out_ps, count(NH * (w.n - 2) + NH))
                    for t in of_half(h):
                        i_ = V.scalar_tensor_tensor(out=yv[:, t, :], in0=yv[:, t, :], scalar=l2mv[:, t, 0:1],
                                                    in1=lnw[:], op0=ALU.subtract, op1=ALU.mult)
                    i_.then_inc(s_l2q, 1)
                    dve.wait_ge(s_l2q, NH * w.n + h + 1)
                    for t in of_half(h):
                        i_ = V.scalar_tensor_tensor(out=t1[w.par][:, t, :], in0=yv[:, t, :], scalar=l2rs[:, t:t + 1],
                                                    in1=x1b[w.par][:, t, :], op0=ALU.mult, op1=ALU.add)
                    i_.then_inc(s_t1, 1)
                    dve.wait_ge(s_t1, NH * w.n + h + 1)
                    token_stats(t1[w.par], l3st, l3mv, h, w, s_l3st, s_l3mv)
                    if h == NH - 1:
                        dve.wait_ge(s_l3mv, NH * w.n + NH)
                        V.tensor_scalar(l3ve[:], l3mv[:, :, 1], LNT_EPS, None, ALU.add).then_inc(s_l3ve, 1)
                        V.tensor_scalar(l3nm[:], l3mv[:, :, 0], -1.0, None, ALU.mult).then_inc(s_l3ve, 1)

                def two_largest():
                    dve.wait_ge(s_wsplit, 1)
                    dve.wait_ge(s_lg, LOGITS * o.n + LOGITS)
                    for t in range(T):
                        i_ = V.max(mx[:, t, :], lg[:, t, :])
                    i_.then_inc(s_mx, 1)
                    dve.wait_ge(s_mx, o.n + 1)
                    V.tensor_tensor(gd[:], mx[:, :, 1], mx[:, :, 0], ALU.subtract).then_inc(s_gd, 1)
                    for t in range(T):
                        i_ = V.max_index(mi[:, t, :], mx[:, t, :], lg[:, t, :])
                    i_.then_inc(s_mi, 1)
                    dve.wait_ge(s_mi, NH * o.n + 1)
                    V.tensor_copy(mf[:].rearrange("p k t -> p t k"), mi[:, :, 0:2]).then_inc(s_mi, 1)

                def gates():
                    def wide(ap):
                        return ap.unsqueeze(2).to_broadcast([P, T, E])

                    g0 = GATE * o.n
                    dve.wait_ge(s_mi, 2 * o.n + 2)
                    V.tensor_tensor(gm1[:], ids[:], wide(mf[:, 0, :]), ALU.is_equal).then_inc(s_gate, 1)
                    V.tensor_tensor(gm2[:], ids[:], wide(mf[:, 1, :]), ALU.is_equal).then_inc(s_gate, 1)
                    dve.wait_ge(s_ge, o.n + 1)
                    V.tensor_scalar(gs[:], ge[:], 1.0, None, ALU.add).then_inc(s_gate, 1)
                    dve.wait_ge(s_gate, g0 + 3)
                    V.reciprocal(g1[:], gs[:]).then_inc(s_gate, 1)
                    dve.wait_ge(s_gate, g0 + 4)
                    V.tensor_tensor(g2[:], ge[:], g1[:], ALU.mult).then_inc(s_gate, 1)
                    V.tensor_tensor(gm1[:], gm1[:], wide(g1[:]), ALU.mult).then_inc(s_gate, 1)
                    dve.wait_ge(s_gate, g0 + 6)
                    V.tensor_tensor(gm2[:], gm2[:], wide(g2[:]), ALU.mult).then_inc(s_gate, 1)
                    dve.wait_ge(s_gate, g0 + 7)
                    V.tensor_tensor(gate[:], gm1[:], gm2[:], ALU.add).then_inc(s_gate, 1)
                    dve.wait_ge(s_gate, g0 + 8)
                    dve.wait_ge(s_gt_ps, NH * o.n)
                    V.tensor_copy(g24[:, :, 0:E], gate[:]).then_inc(s_gate, 1)
                    V.tensor_copy(g24[:, :, 2 * E:3 * E], gate[:]).then_inc(s_gate, 1)
                    dve.wait_ge(s_gate, g0 + 9)
                    V.tensor_tensor(g24[:, :, E:2 * E], gate[:], g24[:, :, 0:E].bitcast(F32),
                                    ALU.subtract).then_inc(s_gate24, 1)

                def gated_bias(h):
                    dve.wait_ge(s_gb_ps, NH * o.n + h + 1)
                    V.tensor_tensor(flat(t1[o.par], h), flat(t1[o.par], h), ps_misc[:], ALU.add).then_inc(s_t1b, 1)

                def gate_experts(g, t):
                    dve.wait_ge(s_gate, GATE * g.n + 8)
                    dve.wait_ge(s_ffn_ps, T * g.n + t + 1)
                    dve.wait_ge(s_t2, count(T * g.n + t - 1))
                    V.tensor_tensor(prod[t % 2][:].rearrange("p (e c) -> p e c", e=E),
                                    ps_ffn[:].rearrange("p (e c) -> p e c", e=E),
                                    gate[:, t, :].unsqueeze(2).to_broadcast([P, E, C]),
                                    ALU.mult).then_inc(s_prod, 1)

                def conv_out(g, h):
                    dve.wait_ge(s_conv_ps, NH * g.n + h + 1)
                    dve.wait_ge(s_x1t_ps, NH * g.n)
                    dve.wait_ge(s_loaded[g.par], 16 * g.nth + 16)
                    V.scalar_tensor_tensor(out=half(x1c, h), in0=ps_conv[:], scalar=cb[:], in1=half(xc[g.par], h),
                                           op0=ALU.add, op1=ALU.add).then_inc(s_x1c, 1)

                def first_stats(h):
                    dve.wait_ge(s_x1t, NH * b.n + h + 1)
                    token_stats(x1t[b.par], l1st, l1mv[b.par], h, b, s_l1st, s_l1mv)

                def first_norms():
                    dve.wait_ge(s_l1mv, NH * b.n + NH)
                    V.tensor_scalar(l1ve[:], l1mv[b.par][:, :, 1], LNT_EPS, None, ALU.add).then_inc(s_l1ve, 1)
                    dve.wait_ge(s_l1ve, b.n + 1)
                    V.reciprocal(l1rec[:], l1ve[:]).then_inc(s_l1q, 1)
                    dve.wait_ge(s_l1q, 3 * b.n + 1)
                    V.scalar_tensor_tensor(out=l1q[:], in0=l1rec[:], scalar=float(C), in1=l1mv[b.par][:, :, 1],
                                           op0=ALU.mult, op1=ALU.mult).then_inc(s_l1q, 1)
                    dve.wait_ge(s_l1q, 3 * b.n + 2)
                    V.tensor_scalar(l1nm[:], l1mv[b.par][:, :, 0], -1.0, None, ALU.mult)
                    V.tensor_scalar(l1n[:], l1q[:], 1e-24, None, ALU.max).then_inc(s_l1q, 1)

                def low_xn(h):
                    dve.wait_ge(s_xnhi, NH * b.n + h + 1)
                    V.tensor_tensor(half(xnlo[b.par], h), ps_misc[:], half(xnhi[b.par], h).bitcast(F32),
                                    ALU.subtract).then_inc(s_xnlo, 1)

                def low_z(h):
                    dve.wait_ge(s_zhi, NH * o.n + h + 1)
                    V.tensor_tensor(half(zlo, h), ps_misc[:], half(zhi, h).bitcast(F32),
                                    ALU.subtract).then_inc(s_zlo, 1)

                if v:
                    dve.wait_ge(s_e_tile, T * v.n + T)
                    dve.wait_ge(s_rb_ps, NH * v.n)
                    V.reciprocal(rinv[:], rsum[v.par][:]).then_inc(s_rinv, 1)
                if w:
                    expm1_tile(w, T - 2)
                    sum_key(w, T - 2)
                if a:
                    dve.wait_ge(s_gmean_ps, a.n + 1)
                    V.tensor_copy(gmean[:], ps_misc[:, 0:1]).then_inc(s_gmeanv, 1)
                    dve.wait_ge(s_gmeanv, GMEAN * a.n + 1)
                    V.tensor_tensor(gdev[:], gmv[:, 0:1], gmean[:], ALU.subtract).then_inc(s_gmeanv, 1)
                    dve.wait_ge(s_gmeanv, GMEAN * a.n + 2)
                    V.scalar_tensor_tensor(out=gv[:], in0=gdev[:], scalar=gdev[:], in1=gmv[:, 1:2],
                                           op0=ALU.mult, op1=ALU.add).then_inc(s_gmeanv, 1)
                if q:
                    gate_experts(q, T - 2)
                if b:
                    conv_out(b, 1)
                if w:
                    low_u(w, T - 2)
                    expm1_tile(w, T - 1)
                if v:
                    scale_rows(0)
                if o:
                    low_z(0)
                if w:
                    sum_key(w, T - 1)
                if q:
                    gate_experts(q, T - 1)
                if o:
                    low_z(1)
                if w:
                    low_u(w, T - 1)
                if v:
                    scale_rows(1)
                    expm1_tile(v, 0)
                if o:
                    dve.wait_ge(s_logit_ps, o.n + 1)
                    logits = ps_misc[:, 0:2 * T * E].rearrange("p (t e) -> p t e", e=2 * E)
                    V.tensor_tensor(lgp[:], logits[:, :, 0:E], rb[:], ALU.add).then_inc(s_lg, 1)
                    dve.wait_ge(s_lg, LOGITS * o.n + 1)
                    V.tensor_tensor(lg[:], logits[:, :, E:2 * E], lgp[:], ALU.add).then_inc(s_lg, 1)
                    two_largest()
                    gates()
                if b:
                    first_stats(0)
                if a:
                    dve.wait_ge(s_gvar_ps, a.n + 1)
                    V.tensor_scalar(gve[:], ps_misc[:, 0:1], GN_EPS, None, ALU.add).then_inc(s_gve, 1)
                if o:
                    gate_experts(o, 0)
                if v:
                    low_u(v, 0)
                if v:
                    scale_rows(2)
                if a:
                    dve.wait_ge(s_grs, a.n + 1)
                    if o:
                        dve.wait_ge(s_z_ps, NH * o.n + NH)
                    V.tensor_scalar(gnf, xc[a.par][:], gmean[:], grs[:], ALU.subtract, ALU.mult).then_inc(s_gnf, 1)
                if v:
                    sum_key(v, 0)
                if b:
                    first_stats(1)
                    first_norms()
                if o:
                    gated_bias(0)
                if v:
                    expm1_tile(v, 1)
                    low_u(v, 1)
                if a:
                    dve.wait_ge(s_gnhi, a.n + 1)
                    V.tensor_tensor(gnlo[:, 1:1 + H, 1:1 + W], rows(gnf),
                                    gnhi[:, 1:1 + H, 1:1 + W].bitcast(F32), ALU.subtract).then_inc(s_gnlo, 1)
                if v:
                    scale_rows(3)
                if w:
                    attention_residual(0)
                if v:
                    sum_key(v, 1)
                if o:
                    gate_experts(o, 1)
                if v:
                    expm1_tile(v, 2)
                    sum_key(v, 2)
                if ahead:
                    dve.wait_ge(s_loaded[ahead.par], 16 * ahead.nth + 16)
                    for h in range(NH):
                        i_ = V.bn_stats(gst[:, h, :], half(xc[ahead.par], h))
                    i_.then_inc(s_gstats, 1)
                if o:
                    gated_bias(1)
                if v:
                    expm1_tile(v, 3)
                if ahead:
                    dve.wait_ge(s_gstats, ahead.n + 1)
                if v:
                    low_u(v, 2)
                if w:
                    attention_residual(1)
                if v:
                    scale_rows(4)
                if w:
                    attention_stats(0)
                if o:
                    gate_experts(o, 2)
                if w:
                    attention_stats(1)
                if v:
                    sum_key(v, 3)
                if v:
                    scale_rows(5)
                    low_u(v, 3)
                if ahead:
                    V.bn_aggr(gmv[:], gst[:].rearrange("p a b -> p (a b)")).then_inc(s_gmv, 1)
                if a:
                    conv_out(a, 0)
                if v:
                    expm1_tile(v, 4)
                if w:
                    residual_norm(0)
                if o:
                    gate_experts(o, 3)
                if v:
                    scale_rows(6)
                    low_u(v, 4)
                if b:
                    low_xn(0)
                if v:
                    sum_key(v, 4)
                if w:
                    residual_norm(1)
                if v:
                    expm1_tile(v, 5)
                if o:
                    gate_experts(o, 4)
                if v:
                    scale_rows(7)
                    low_u(v, 5)
                    sum_key(v, 5)
                if o:
                    gate_experts(o, 5)
                if b:
                    low_xn(1)

            iterations(dve, NB, run)


def kernel(x, L0_conv_weight, L0_conv_bias, L1_attn_ln_weight, L1_attn_ln_bias,
           L1_ffn_router_w, L1_ffn_router_b, L1_ffn_expert_w, L1_ffn_expert_b):
    import numpy as np
    import concourse.bacc as bacc
    from concourse.bass_utils import run_bass_kernel_spmd

    x = np.asarray(x)
    nb, c, h, w = x.shape
    tiles = h * w // P
    experts = L1_ffn_expert_b.shape[0]
    conv_weight, expert_weight = np.asarray(L0_conv_weight), np.asarray(L1_ffn_expert_w)
    group = c // 32
    same_group = np.arange(c)[:, None] // group == np.arange(c)[None, :] // group
    bias_rows = np.zeros((3 * experts, 2), np.float32)
    bias_rows[:2 * experts, 0] = 1
    bias_rows[2 * experts:, 1] = 1
    arrays = {
        "x": x.reshape(nb, c, h * w),
        "conv_w": conv_weight.transpose(1, 2, 3, 0).reshape(c, -1),
        "conv_b": np.asarray(L0_conv_bias).reshape(c, 1),
        "ln_w": np.broadcast_to(np.asarray(L1_attn_ln_weight), (P, c)),
        "ln_b": np.broadcast_to(np.asarray(L1_attn_ln_bias), (P, c)),
        "router_w": np.asarray(L1_ffn_router_w),
        "router_b": np.broadcast_to(np.asarray(L1_ffn_router_b), (P, tiles, experts)),
        "expert_w": expert_weight.transpose(1, 0, 2).reshape(c, -1),
        "expert_b": np.concatenate([np.asarray(L1_ffn_expert_b)] * 3),
        "identity": np.eye(P, dtype=np.float32),
        "group_mean": same_group.astype(np.float32) / np.float32(group),
        "expert_ids": np.broadcast_to(np.arange(experts, dtype=np.float32), (P, tiles, experts)),
        "bias_rows": bias_rows,
    }
    arrays = {k: np.ascontiguousarray(a) for k, a in arrays.items()}
    nc = bacc.Bacc("TRN2", target_bir_lowering=False, num_devices=1)
    aps = {k: nc.dram_tensor(k, a.shape, F32, kind="ExternalInput").ap() for k, a in arrays.items()}
    out = nc.dram_tensor("out", (nb, c, h * w), F32, kind="ExternalOutput").ap()
    build(nc, out=out, **aps)
    result = run_bass_kernel_spmd(nc, [arrays], core_ids=[0])
    return result.results[0]["out"].reshape(nb, c, h, w)
```
